# Optimizing a Trainium2 kernel written in Bass

```python
import numpy as np
import jax
import jax.numpy as jnp

def _softmax(x, axis=-1):
    return jax.nn.softmax(x, axis=axis)

def _gelu(x):
    return jax.nn.gelu(x, approximate=True)

def _silu(x):
    return jax.nn.silu(x)

def _sigmoid(x):
    return jax.nn.sigmoid(x)

def _layernorm(x, axis=-1, eps=1e-05):
    m = jnp.mean(x, axis=axis, keepdims=True)
    v = jnp.var(x, axis=axis, keepdims=True)
    return (x - m) / jnp.sqrt(v + eps)

def _scatter_add(tgt, idx, src, axis=0):
    return tgt.at[idx].add(src)

def _segment_sum(src, seg, n):
    return jax.ops.segment_sum(src, seg, n)
kernel_name = 'mk_lm_tower_d1_tok_ids1024_r4_bf1a18'

def setup_inputs(seed: int=0):
    np.random.seed(seed)
    _w = jnp.asarray

    def _rec_inputs():
        import jax
        import jax.numpy as jnp
        _rk = jax.random.key(seed)
        x = jax.random.randint(jax.random.fold_in(_rk, 1), (4, 1024), 0, 12564, jnp.int32)
        return x
    x = _rec_inputs()

    def _L0_tok_setup():
        import jax, jax.numpy as jnp
        import numpy as np
        D_M = 256
        VOCAB = 50257
        BASE = 10000.0
        B, S = (8, 1024)

        def _positional_encoding(seq_len, d_m, base, dtype):
            pos = jnp.arange(seq_len, dtype=dtype)
            i = jnp.arange(d_m // 2, dtype=dtype)
            inv_freq = jnp.power(jnp.asarray(base, dtype), -2.0 * i / d_m)
            ang = pos[:, None] * inv_freq[None, :]
            pe = jnp.stack([jnp.sin(ang), jnp.cos(ang)], axis=-1)
            return pe.reshape(seq_len, d_m)
        key = jax.random.key(seed)
        k1, k2 = jax.random.split(key)
        x = jax.random.randint(k1, (B, S), 0, VOCAB, dtype=jnp.int64)
        emb_table = jax.random.normal(k2, (VOCAB, D_M), dtype=jnp.float32)
        return {'x': x, 'emb_table': emb_table}
    _L0_tok_all = _L0_tok_setup()
    _L0_tok_in = {k: v for k, v in _L0_tok_all.items() if k in ('emb_table',)}
    del _L0_tok_all

    def _L0_attn_setup():
        import jax, jax.numpy as jnp
        import numpy as np
        D_MODEL = 256
        NHEAD = 16
        HID = int(D_MODEL * 4.0 * (2.0 / 3.0))
        EPS = 1e-05

        def _ln(x, w, b):
            m = jnp.mean(x, axis=-1, keepdims=True)
            v = jnp.mean((x - m) ** 2, axis=-1, keepdims=True)
            return (x - m) / jnp.sqrt(v + EPS) * w + b
        key = jax.random.key(seed)
        ks = jax.random.split(key, 10)
        w = lambda k, shape: jax.random.normal(k, shape, jnp.float32) * 0.02
        D = D_MODEL
        inp = {'x': jax.random.normal(ks[0], (1, 512, D), jnp.float32), 'norm1_w': jnp.ones((D,), jnp.float32), 'norm1_b': jnp.zeros((D,), jnp.float32), 'wq': w(ks[1], (D, D)), 'bq': jnp.zeros((D,), jnp.float32), 'wk': w(ks[2], (D, D)), 'bk': jnp.zeros((D,), jnp.float32), 'wv': w(ks[3], (D, D)), 'bv': jnp.zeros((D,), jnp.float32), 'wg': w(ks[4], (D, D)), 'bg': jnp.zeros((D,), jnp.float32), 'wo': w(ks[5], (D, D)), 'bo': jnp.zeros((D,), jnp.float32), 'gn_w': jnp.ones((D,), jnp.float32), 'gn_b': jnp.zeros((D,), jnp.float32), 'norm2_w': jnp.ones((D,), jnp.float32), 'norm2_b': jnp.zeros((D,), jnp.float32), 'w_in': w(ks[6], (D, 2 * HID)), 'b_in': jnp.zeros((2 * HID,), jnp.float32), 'w_out': w(ks[7], (HID, D)), 'b_out': jnp.zeros((D,), jnp.float32)}
        return inp
    _L0_attn_all = _L0_attn_setup()
    _L0_attn_in = {k: v for k, v in _L0_attn_all.items() if k in ('norm1_w', 'norm1_b', 'wq', 'bq', 'wk', 'bk', 'wv', 'bv', 'wg', 'bg', 'wo', 'bo', 'gn_w', 'gn_b', 'norm2_w', 'norm2_b', 'w_in', 'b_in', 'w_out', 'b_out')}
    del _L0_attn_all

    def _L0_ffn_setup():
        import jax, jax.numpy as jnp
        import numpy as np
        import math
        E = 32
        K = 2
        CF = 1.2
        D = 256
        F = 1024
        key = jax.random.key(seed)
        ks = jax.random.split(key, 7)
        s = 0.02
        return {'x': jax.random.normal(ks[0], (4, 512, D), jnp.float32), 'gate_w': jax.random.normal(ks[1], (D, E), jnp.float32) * s, 'gate_b': jnp.zeros((E,), jnp.float32), 'w1': jax.random.normal(ks[2], (E, D, F), jnp.float32) * s, 'b1': jnp.zeros((E, F), jnp.float32), 'w2': jax.random.normal(ks[3], (E, F, D), jnp.float32) * s, 'b2': jnp.zeros((E, D), jnp.float32)}
    _L0_ffn_all = _L0_ffn_setup()
    _L0_ffn_in = {k: v for k, v in _L0_ffn_all.items() if k in ('gate_w', 'gate_b', 'w1', 'b1', 'w2', 'b2')}
    del _L0_ffn_all
    return {'x': x, 'L0_tok_emb_table': _L0_tok_in['emb_table'], 'L0_attn_norm1_w': _L0_attn_in['norm1_w'], 'L0_attn_norm1_b': _L0_attn_in['norm1_b'], 'L0_attn_wq': _L0_attn_in['wq'], 'L0_attn_bq': _L0_attn_in['bq'], 'L0_attn_wk': _L0_attn_in['wk'], 'L0_attn_bk': _L0_attn_in['bk'], 'L0_attn_wv': _L0_attn_in['wv'], 'L0_attn_bv': _L0_attn_in['bv'], 'L0_attn_wg': _L0_attn_in['wg'], 'L0_attn_bg': _L0_attn_in['bg'], 'L0_attn_wo': _L0_attn_in['wo'], 'L0_attn_bo': _L0_attn_in['bo'], 'L0_attn_gn_w': _L0_attn_in['gn_w'], 'L0_attn_gn_b': _L0_attn_in['gn_b'], 'L0_attn_norm2_w': _L0_attn_in['norm2_w'], 'L0_attn_norm2_b': _L0_attn_in['norm2_b'], 'L0_attn_w_in': _L0_attn_in['w_in'], 'L0_attn_b_in': _L0_attn_in['b_in'], 'L0_attn_w_out': _L0_attn_in['w_out'], 'L0_attn_b_out': _L0_attn_in['b_out'], 'L0_ffn_gate_w': _L0_ffn_in['gate_w'], 'L0_ffn_gate_b': _L0_ffn_in['gate_b'], 'L0_ffn_w1': _L0_ffn_in['w1'], 'L0_ffn_b1': _L0_ffn_in['b1'], 'L0_ffn_w2': _L0_ffn_in['w2'], 'L0_ffn_b2': _L0_ffn_in['b2']}

def reference(x, L0_tok_emb_table, L0_attn_norm1_w, L0_attn_norm1_b, L0_attn_wq, L0_attn_bq, L0_attn_wk, L0_attn_bk, L0_attn_wv, L0_attn_bv, L0_attn_wg, L0_attn_bg, L0_attn_wo, L0_attn_bo, L0_attn_gn_w, L0_attn_gn_b, L0_attn_norm2_w, L0_attn_norm2_b, L0_attn_w_in, L0_attn_b_in, L0_attn_w_out, L0_attn_b_out, L0_ffn_gate_w, L0_ffn_gate_b, L0_ffn_w1, L0_ffn_b1, L0_ffn_w2, L0_ffn_b2):
    import jax
    import jax.numpy as jnp

    def _L0_tok_ref(x, emb_table):
        import jax, jax.numpy as jnp
        import numpy as np
        D_M = 256
        VOCAB = 50257
        BASE = 10000.0
        B, S = (8, 1024)

        def _positional_encoding(seq_len, d_m, base, dtype):
            pos = jnp.arange(seq_len, dtype=dtype)
            i = jnp.arange(d_m // 2, dtype=dtype)
            inv_freq = jnp.power(jnp.asarray(base, dtype), -2.0 * i / d_m)
            ang = pos[:, None] * inv_freq[None, :]
            pe = jnp.stack([jnp.sin(ang), jnp.cos(ang)], axis=-1)
            return pe.reshape(seq_len, d_m)
        emb = emb_table[x]
        pe = _positional_encoding(x.shape[1], emb_table.shape[1], BASE, emb_table.dtype)
        return emb + pe[None, :, :]

    def _L0_attn_ref(x, norm1_w, norm1_b, wq, bq, wk, bk, wv, bv, wg, bg, wo, bo, gn_w, gn_b, norm2_w, norm2_b, w_in, b_in, w_out, b_out):
        import jax, jax.numpy as jnp
        import numpy as np
        D_MODEL = 256
        NHEAD = 16
        HID = int(D_MODEL * 4.0 * (2.0 / 3.0))
        EPS = 1e-05

        def _ln(x, w, b):
            m = jnp.mean(x, axis=-1, keepdims=True)
            v = jnp.mean((x - m) ** 2, axis=-1, keepdims=True)
            return (x - m) / jnp.sqrt(v + EPS) * w + b
        B, S, D = x.shape
        H = NHEAD
        hd = D // H
        xn = _ln(x, norm1_w, norm1_b)
        q = (xn @ wq + bq).reshape(B, S, H, hd).transpose(0, 2, 1, 3)
        k = (xn @ wk + bk).reshape(B, S, H, hd).transpose(0, 2, 1, 3)
        v = (xn @ wv + bv).reshape(B, S, H, hd).transpose(0, 2, 1, 3)
        gamma = 1.0 - jnp.exp2(-5.0 - jnp.arange(H, dtype=jnp.float32))
        n = jnp.arange(S)
        diff = (n[:, None] - n[None, :]).astype(jnp.float32)
        Dmat = jnp.where(diff >= 0, jnp.exp(jnp.log(gamma)[:, None, None] * diff), 0.0)
        scores = jnp.einsum('bhnd,bhmd->bhnm', q, k) * hd ** (-0.5)
        ret = jnp.einsum('bhnm,bhmd->bhnd', scores * Dmat, v)
        ret = ret.transpose(0, 2, 1, 3)
        mu = jnp.mean(ret, axis=-1, keepdims=True)
        var = jnp.mean((ret - mu) ** 2, axis=-1, keepdims=True)
        gn = ((ret - mu) / jnp.sqrt(var + EPS)).reshape(B, S, D) * gn_w + gn_b
        gate = jax.nn.silu(xn @ wg + bg)
        h = gate * gn @ wo + bo
        x = x + h
        x2 = _ln(x, norm2_w, norm2_b)
        uv = x2 @ w_in + b_in
        u, g = jnp.split(uv, 2, axis=-1)
        x = x + (jax.nn.silu(u) * g @ w_out + b_out)
        return x

    def _L0_ffn_ref(x, gate_w, gate_b, w1, b1, w2, b2):
        import jax, jax.numpy as jnp
        import numpy as np
        import math
        E = 32
        K = 2
        CF = 1.2
        D = 256
        F = 1024
        orig_shape = x.shape
        xt = x.reshape(-1, D)
        T = xt.shape[0]
        C = int(math.ceil(T * K / E * CF))
        logits = xt @ gate_w + gate_b
        probs = jax.nn.softmax(logits, axis=-1)
        top_w, top_i = jax.lax.top_k(probs, K)
        w = top_w / jnp.sum(top_w, axis=-1, keepdims=True)
        flat_e = top_i.reshape(-1)
        oh = jax.nn.one_hot(flat_e, E, dtype=jnp.int32)
        pos_all = jnp.cumsum(oh, axis=0) - 1
        pos = jnp.take_along_axis(pos_all, flat_e[:, None], axis=1)[:, 0]
        valid = pos < C
        pos_d = jnp.where(valid, pos, C)
        x_rep = jnp.repeat(xt, K, axis=0)
        xe = jnp.zeros((E, C, D), x.dtype).at[flat_e, pos_d].add(x_rep, mode='drop')
        he = jax.nn.gelu(jnp.einsum('ecd,edf->ecf', xe, w1) + b1[:, None, :], approximate=False)
        ye = jnp.einsum('ecf,efd->ecd', he, w2) + b2[:, None, :]
        y_flat = ye[flat_e, jnp.minimum(pos, C - 1)] * valid[:, None].astype(x.dtype)
        y = (y_flat.reshape(T, K, D) * w[..., None]).sum(axis=1)
        return y.reshape(orig_shape)
    h = _L0_tok_ref(x, L0_tok_emb_table)
    h = h + _L0_attn_ref(_layernorm(h, axis=-1), L0_attn_norm1_w, L0_attn_norm1_b, L0_attn_wq, L0_attn_bq, L0_attn_wk, L0_attn_bk, L0_attn_wv, L0_attn_bv, L0_attn_wg, L0_attn_bg, L0_attn_wo, L0_attn_bo, L0_attn_gn_w, L0_attn_gn_b, L0_attn_norm2_w, L0_attn_norm2_b, L0_attn_w_in, L0_attn_b_in, L0_attn_w_out, L0_attn_b_out)
    h = h + _L0_ffn_ref(_layernorm(h, axis=-1), L0_ffn_gate_w, L0_ffn_gate_b, L0_ffn_w1, L0_ffn_b1, L0_ffn_w2, L0_ffn_b2)
    return h

_drawn_inputs = setup_inputs


def setup_inputs(seed=0):
    import zlib

    import numpy as np

    out = dict(_drawn_inputs(seed))
    spreads = {'L0_attn_norm1_w': (1.0, 0.6),
     'L0_attn_norm1_b': (0.0, 0.746),
     'L0_attn_bq': (0.0, 0.648),
     'L0_attn_bk': (0.0, 0.456),
     'L0_attn_bv': (0.0, 0.503),
     'L0_attn_bg': (0.0, 0.8),
     'L0_attn_bo': (0.0, 0.1),
     'L0_attn_gn_w': (1.0, 0.6),
     'L0_attn_gn_b': (0.0, 0.8),
     'L0_attn_norm2_w': (1.0, 0.6),
     'L0_attn_norm2_b': (0.0, 0.8),
     'L0_attn_b_in': (0.0, 0.8),
     'L0_attn_b_out': (0.0, 0.371),
     'L0_ffn_gate_b': (0.0, 0.1),
     'L0_ffn_b1': (0.0, 0.795),
     'L0_ffn_b2': (0.0, 0.285)}
    factors = {'L0_attn_w_in': 3.339, 'L0_attn_w_out': 3.282, 'L0_ffn_w1': 3.925}
    for name, (base, spread) in spreads.items():
        noise = np.random.default_rng([zlib.crc32(name.encode()), seed]).standard_normal(out[name].shape)
        drawn = base * np.exp(spread * noise) if base else spread * noise
        out[name] = jnp.asarray(drawn.astype(out[name].dtype))
    for name, factor in factors.items():
        out[name] = (out[name] * factor).astype(out[name].dtype)
    return out
```

```python
import concourse.bass as bass
from concourse import mybir
from contextlib import ExitStack
import numpy as np

f32 = mybir.dt.float32
bf16 = mybir.dt.bfloat16
i32 = mybir.dt.int32
u32 = mybir.dt.uint32
ALU = mybir.AluOpType
ACT = mybir.ActivationFunctionType
AX = mybir.AxisListType

P = 128
B, S, D = 4, 1024, 256
T = B * S
KD = D // P
H, HD = 16, 16
J = 4
GT = J * P
G = T // GT
HID = 682
NH = -(-HID // P)
HW = [min(P, HID - n * P) for n in range(NH)]
E, F, C = 32, 1024, 308
MF = F // P
SP_ = 104
SJ = 3
CP = SP_ * SJ
ROW = D + 2
EPS = 1e-5
DUMP = CP

V_N1W, V_N1B, V_BQ, V_BK, V_BG, V_GNW, V_GNB, V_N2W, V_N2B = range(0, 18, 2)
V_BU = 18
V_BGL = V_BU + NH
V_ALL = V_BGL + NH

K_PE = 0
K_Q = K_PE + 8 * D
K_K = K_Q + KD * P
K_BD = K_K + KD * P
K_CAUSAL = K_BD + KD * P
K_ID = K_CAUSAL + P
K_STRICT = K_ID + P
K_IOTA = K_STRICT + P
K_TOK = K_IOTA + E
K_PAR = K_TOK + 8
K_ALL = K_PAR + 2


def shape_constants():
    c = np.zeros((P, K_ALL), np.float32)
    p = np.arange(P)
    pos = np.arange(S, dtype=np.float32)
    inv = np.power(np.float32(10000.0), (np.float32(-2.0) * np.arange(D // 2, dtype=np.float32) / np.float32(D))).astype(np.float32)
    ang = (pos[:, None] * inv[None, :]).astype(np.float32).astype(np.float64)
    pe = np.stack([np.sin(ang), np.cos(ang)], -1).reshape(S, D)
    c[:, K_PE:K_Q] = pe.reshape(8, P, D).transpose(1, 0, 2).reshape(P, -1)
    gamma = 1.0 - 2.0 ** (-5.0 - np.arange(H))
    feature = np.arange(D).reshape(KD, P)
    gf = gamma[feature // HD].T
    c[:, K_Q:K_K] = (HD ** -0.5 * gf[:, :, None] ** p[None, None, :]).reshape(P, -1)
    c[:, K_K:K_BD] = (gf[:, :, None] ** -p[None, None, :].astype(np.float64)).reshape(P, -1)
    same = (p[:, None] // HD == p[None, :] // HD)
    c[:, K_BD:K_CAUSAL] = (gf[:, :, None] ** P * same[:, None, :]).reshape(P, -1)
    c[:, K_CAUSAL:K_ID] = p[:, None] <= p[None, :]
    c[:, K_ID:K_STRICT] = np.eye(P)
    c[:, K_STRICT:K_IOTA] = p[:, None] < p[None, :]
    c[:, K_IOTA:K_TOK] = np.arange(E)[None, :]
    c[:, K_TOK:K_PAR] = (np.arange(J)[None, :, None] * P + p[:, None, None] + np.zeros((1, 1, 2))).reshape(P, -1)
    c[:, K_PAR] = (p // HD) % 2 == 0
    c[:, K_PAR + 1] = (p // HD) % 2 == 1
    empty = np.zeros((SP_, SJ, ROW), np.float32)
    empty[:, :, D] = (T + np.arange(CP, dtype=np.int32).reshape(SP_, SJ)).astype(np.int32).view(np.float32)
    return c, empty


def build(nc, idx, emb, consts, empty, vecs, rows, wq, wk, wv, wg, wo, w_in, w_out, gate_w, gate_b, w1, b1, w2, b2,
          out, xe):
    ctx = ExitStack()
    with ctx:
        def sb(name, shape, dt=f32):
            return ctx.enter_context(nc.sbuf_tensor(name, shape, dt))

        def sem(name):
            return ctx.enter_context(nc.semaphore(name))

        const = sb("const", [P, K_ALL])
        vec = sb("vec", [P, V_ALL])
        row = sb("row", [P, 3, D])
        gb = sb("gb", [P, E])
        Wq, Wk, Wv, Wg, Wo = (sb(n, [P, KD, D]) for n in ("Wq", "Wk", "Wv", "Wg", "Wo"))
        Win = sb("Win", [P, KD, 2 * HID])
        Wout = sb("Wout", [P, NH, D])
        Gw = sb("Gw", [P, KD, E])
        strict = sb("strict", [P, P], bf16)
        ones = sb("ones", [P, P], bf16)
        half = sb("half", [P, 64])
        euler = sb("euler", [P, J])
        emptyrow = sb("emptyrow", [SP_, SJ * ROW])
        B1 = sb("B1", [P, E, MF])
        B2 = sb("B2", [P, E, KD])

        pe_tab = const[:, K_PE:K_Q].rearrange("p (c d) -> p c d", d=D)
        q_tab = const[:, K_Q:K_K].rearrange("p (m n) -> p m n", m=KD)
        k_tab = const[:, K_K:K_BD].rearrange("p (m n) -> p m n", m=KD)
        bd_tab = const[:, K_BD:K_CAUSAL]
        causal = const[:, K_CAUSAL:K_ID]
        ident = const[:, K_ID:K_STRICT]
        iota = const[:, K_IOTA:K_TOK]
        tok0 = const[:, K_TOK:K_PAR]

        idxg = sb("idxg", [P, J], i32)
        emb_in = sb("emb_in", [P, J, D])
        hres = [sb(f"hres{n}", [P, J, D]) for n in range(2)]
        a = [sb(f"a{n}", [P, J, D]) for n in range(2)]
        an = sb("an", [P, J, D])
        xnT = sb("xnT", [P, KD, GT])
        qT = sb("qT", [P, KD, GT])
        kT = sb("kT", [P, KD, GT])
        kX = sb("kX", [P, 2, KD, GT])
        gateT = sb("gateT", [P, KD, GT])
        v = sb("v", [P, J, D])
        ktok = sb("ktok", [P, J, D])
        sm = sb("sm", [P, J, 4, P])
        state = sb("state", [P, KD * P])
        stmp = sb("stmp", [P, KD * P])
        ret = sb("ret", [P, J, D])
        sq = sb("sq", [P, 2, D])
        gn = sb("gn", [P, J, D])
        gnT = sb("gnT", [P, KD, GT])
        x2n = sb("x2n", [P, J, D])
        x2T = sb("x2T", [P, KD, GT])
        su = sb("su", [P, 2, GT])
        prodT = sb("prodT", [P, NH, GT])
        hf = sb("hf", [P, J, D])
        pl = sb("pl", [P, J, 2, ROW])
        xtT = sb("xtT", [P, KD, GT])
        lgs = sb("lgs", [P, J, E])
        oh = sb("oh", [P, J * 2, E])
        ohc = sb("ohc", [P, J * 2, E])
        osum = sb("osum", [P, J, E], bf16)
        oacc = sb("oacc", [P, E], bf16)
        osg = sb("osg", [P, E])
        slot = sb("slot", [P, J * 2], i32)
        tokf = sb("tokf", [P, J * 2])
        m8 = sb("m8", [P, J, 8])
        i8 = sb("i8", [P, J, 8], u32)
        idf = sb("idf", [P, J, 2])
        small = sb("small", [P, 512])
        off = [0]

        def tiny(n):
            off[0] += n
            return small[:, off[0] - n:off[0]]

        st_h, st_2, st_3 = (tiny(24).rearrange("p (j n) -> p j n", j=J) for _ in range(3))
        mv_h, mv_2, mv_3 = (tiny(8).rearrange("p (j n) -> p j n", j=J) for _ in range(3))
        ve_h, r1, va_h, r2, ve_2, r_2, ve_3, r_3, dl, ed, den, wt1 = (tiny(J) for _ in range(12))
        gsum, gvar, grst = (tiny(64) for _ in range(3))
        pos, slf, over = (tiny(J * 2) for _ in range(3))

        W1 = [sb(f"W1{n}", [P, KD, F]) for n in range(2)]
        W2 = [sb(f"W2{n}", [P, MF, D]) for n in range(2)]
        xr = [kX[0:SP_, n, :, :].rearrange("p k n -> p (k n)")[:, 0:SJ * ROW].rearrange("p (j n) -> p j n", j=SJ)
              for n in range(2)]
        xeT = [t[:, :, 0:CP] for t in (qT, kT)]
        heT = prodT[:, :, :].rearrange("p n t -> p (n t)")[:, 0:MF * CP].rearrange("p (m c) -> p m c", m=MF)
        yT = v[:, :, :].rearrange("p j d -> p (j d)")[:, 0:KD * CP].rearrange("p (k c) -> p k c", k=KD)
        yw = ktok[0:SP_, 0:SJ, :]

        bank = [ctx.enter_context(nc.psum_tensor(f"bank{n}", [P, 512], f32)) for n in range(8)]

        in_small, in_w, in_ffn, in_moe, in_empty = (sem(n) for n in ("in_small", "in_w", "in_ffn", "in_moe", "in_empty"))
        consts_set = sem("consts_set")
        strict_set = sem("strict_set")
        passed = sem("passed")
        slots_empty = sem("slots_empty")
        idx_in, emb_landed = sem("idx_in"), sem("emb_landed")
        h_set, stats_h, ve_h_set, va_h_set, r1_set, r2_set, a_set, an_set, abo_set = (
            sem(n) for n in ("h_set", "stats_h", "ve_h_set", "va_h_set", "r1_set", "r2_set", "a_set", "an_set", "abo_set"))
        xT_full, xT_taken = sem("xT_full"), sem("xT_taken")
        qk_full, qk_taken = sem("qk_full"), sem("qk_taken")
        gate_full, gate_taken = sem("gate_full"), sem("gate_taken")
        v_full, v_taken = sem("v_full"), sem("v_taken")
        kt_full, kt_taken = sem("kt_full"), sem("kt_taken")
        kX_set = sem("kX_set")
        sc_full, sc_masked = sem("sc_full"), sem("sc_masked")
        kv_full, kv_added, state_set = sem("kv_full"), sem("kv_added"), sem("state_set")
        ret_full, ret_taken = sem("ret_full"), sem("ret_taken")
        gsum_set, xc_set, sq_set, gvar_set, gve_set, grst_set, gn_set = (
            sem(n) for n in ("gsum_set", "xc_set", "sq_set", "gvar_set", "gve_set", "grst_set", "gn_set"))
        gnT_full, gnT_taken, gg_set = sem("gnT_full"), sem("gnT_taken"), sem("gg_set")
        wo_full, wo_taken = sem("wo_full"), sem("wo_taken")
        stats_2, ve_2_set, r_2_set, x2n_set = (sem(n) for n in ("stats_2", "ve_2_set", "r_2_set", "x2n_set"))
        x2T_full, x2T_taken = sem("x2T_full"), sem("x2T_taken")
        u_full, u_taken, g_full, prod_set = sem("u_full"), sem("u_taken"), sem("g_full"), sem("prod_set")
        hx_add, hx_set = sem("hx_add"), sem("hx_set")
        o_full, hf_set, out_done = sem("o_full"), sem("hf_set"), sem("out_done")
        stats_3, ve_3_set, r_3_set, xt_set = (sem(n) for n in ("stats_3", "ve_3_set", "r_3_set", "xt_set"))
        xtT_full, xtT_taken = sem("xtT_full"), sem("xtT_taken")
        lg_full, lg_taken = sem("lg_full"), sem("lg_taken")
        top_set, dl_set, ed_set, oh_set, osum_set = (sem(n) for n in ("top_set", "dl_set", "ed_set", "oh_set", "osum_set"))
        route = sem("route")
        cnt_full, cnt_taken = sem("cnt_full"), sem("cnt_taken")
        oacc_set, slot_set, wt_set = sem("oacc_set"), sem("slot_set"), sem("wt_set")
        scattered = sem("scattered")
        bn = sem("bn")
        w1_in = [sem(f"w1_in{n}") for n in range(2)]
        w2_in = [sem(f"w2_in{n}") for n in range(2)]
        xr_in = [sem(f"xr_in{n}") for n in range(2)]
        xeT_full, xeT_taken = sem("xeT_full"), sem("xeT_taken")
        h1_full, h1_taken = sem("h1_full"), sem("h1_taken")
        y_full, y_taken = sem("y_full"), sem("y_taken")
        yt_full, yt_taken = sem("yt_full"), sem("yt_taken")
        added = sem("added")

        block = ctx.enter_context(nc.Block())

        def wait(eng, s, n):
            if isinstance(n, int) and n <= 0:
                return
            eng.wait_ge(s, n)

        def wait_apart(eng, s, n):
            wait(eng, s, n)
            if not isinstance(n, int):
                eng.sem_inc(passed, 1)

        def steps(eng, step):
            step(0, 0, True, False, True, 0)
            with eng.Fori(0, (G - 2) // 2) as i:
                for r in range(2):
                    step(i * 2 + (1 + r), (1 + r) % 2, True, True, True, i + r)
            step(G - 1, 1, True, True, False, G // 2 - 1)
            step(G, 0, False, True, False, G // 2)

        def experts(eng, part):
            part(0, 0, True, False, 1)
            part(1, 1, False, False, 1)
            with eng.Fori(0, (E - 4) // 2) as i:
                for r in range(2):
                    part(i * 2 + (2 + r), r, False, False, i + 2)
            part(E - 2, 0, False, False, E // 2)
            part(E - 1, 1, False, True, E // 2)

        @block.sync
        def _(sp):
            sp.dma_start(const[:, :], consts).then_inc(in_small, 16)
            sp.dma_start(vec[:, :], vecs).then_inc(in_small, 16)
            sp.dma_start(row[:, :, :], rows.partition_broadcast(P)).then_inc(in_small, 16)
            sp.dma_start(gb[:, :], gate_b.partition_broadcast(P)).then_inc(in_small, 16)
            sp.dma_start(Gw[:, :, :], gate_w.rearrange("(k p) n -> p k n", p=P)).then_inc(in_small, 16)
            for dst, src in ((Wq, wq), (Wk, wk), (Wg, wg), (Wv, wv), (Wo, wo)):
                sp.dma_start(dst[:, :, :], src.rearrange("(k p) n -> p k n", p=P)).then_inc(in_w, 16)
            sp.dma_start(Win[:, :, :], w_in.rearrange("(k p) n -> p k n", p=P)).then_inc(in_ffn, 16)
            full = HID // P
            sp.dma_start(Wout[:, 0:full, :], w_out[0:full * P, :].rearrange("(k p) n -> p k n", p=P)).then_inc(in_ffn, 16)
            sp.dma_start(Wout[0:HID - full * P, full, :], w_out[full * P:HID, :]).then_inc(in_ffn, 16)
            sp.dma_start(emptyrow[:, :], empty.rearrange("p j n -> p (j n)")).then_inc(in_empty, 16)
            sp.wait_ge(in_empty, 16)
            sp.dma_start(xe.rearrange("(e p j) n -> p e (j n)", e=E, p=SP_),
                         emptyrow[:, :].unsqueeze(1).to_broadcast([SP_, E, SJ * ROW])).then_inc(slots_empty, 16)
            sp.dma_start(B1[:, :, :], b1).then_inc(in_moe, 16)
            sp.dma_start(B2[:, :, :], b2).then_inc(in_moe, 16)
            for n in range(2):
                sp.dma_start(W1[n][:, :, :], w1[n]).then_inc(w1_in[n], 16)
                sp.dma_start(W2[n][:, :, :], w2[n]).then_inc(w2_in[n], 16)

            out_g = out[0:T, :].rearrange("(g j p) d -> g p j d", j=J, p=P)

            def step(s, par, first, second, ahead, seq):
                if second:
                    wait(sp, hf_set, 2 * s)
                    sp.dma_start(out_g[s - 1], hf[:, :, :]).then_inc(out_done, 16)
            steps(sp, step)

            sp.dma_start(out[T:T + DUMP, :].rearrange("(p j) d -> p (j d)", p=SP_), emptyrow[:, 0:SJ * D]).then_inc(out_done, 16)

            sp.wait_ge(scattered, 16 * 2 * J * G)
            xe_e = xe.rearrange("(e p j) n -> e p j n", e=E, p=SP_)

            def part(e, b, first, last, n):
                if first:
                    for x in range(2):
                        sp.dma_start(xr[x], xe_e[x]).then_inc(xr_in[x], 16)
                    return
                if last:
                    return
                wait(sp, y_full, 2 * e)
                sp.dma_start(W1[1 - b][:, :, :], w1[e + 1]).then_inc(w1_in[1 - b], 16)
                sp.dma_start(W2[1 - b][:, :, :], w2[e + 1]).then_inc(w2_in[1 - b], 16)
                wait(sp, added, 16 * SJ * e)
                sp.dma_start(xr[1 - b], xe_e[e + 1]).then_inc(xr_in[1 - b], 16)
            experts(sp, part)
            sp.wait_ge(out_done, 16 * (G + 1))

        @block.gpsimd
        def _(pool):
            pool.memset(half[:, :], -0.5).then_inc(consts_set, 1)
            pool.memset(euler[:, :], float(np.e)).then_inc(consts_set, 1)
            pool.memset(ones[:, :], 1.0).then_inc(consts_set, 1)
            pool.memset(oacc[:, :], 0.0).then_inc(consts_set, 1)
            pool.wait_ge(consts_set, 4)
            pool.wait_ge(in_small, 16 * 5)

            def gather(g):
                wait_apart(pool, h_set, g)
                pool.dma_start(idxg[:, :], idx[g]).then_inc(idx_in, 16)
                wait_apart(pool, idx_in, 16 * (g + 1))
                for j in range(J):
                    pool.indirect_dma_start(emb_in[:, j, :], None, emb,
                                            bass.IndirectOffsetOnAxis(ap=idxg[:, j:j + 1], axis=0)).then_inc(emb_landed, 16)

            def head(g, par):
                wait_apart(pool, emb_landed, 16 * J * (g + 1))
                pool.tensor_tensor(hres[par][:, :, :], emb_in[:, :, :], pe_tab[:, J * par:J * par + J, :],
                                   ALU.add).then_inc(h_set, 1)

            def head_roots(g, par):
                wait_apart(pool, stats_h, g + 1)
                pool.tensor_scalar(ve_h, mv_h[:, :, 1], EPS, None, ALU.add).then_inc(ve_h_set, 1)
                wait_apart(pool, ve_h_set, g + 1)
                pool.tensor_tensor(r1, ve_h, half[:, 0:J], ALU.pow).then_inc(r1_set, 1)
                wait_apart(pool, r1_set, g + 1)
                pool.tensor_tensor(va_h, r1, r1, ALU.mult).then_inc(va_h_set, 1)
                wait_apart(pool, va_h_set, 3 * g + 1)
                pool.tensor_tensor(va_h, va_h, mv_h[:, :, 1], ALU.mult).then_inc(va_h_set, 1)
                wait_apart(pool, va_h_set, 3 * g + 2)
                pool.tensor_scalar(va_h, va_h, EPS, None, ALU.add).then_inc(va_h_set, 1)
                wait_apart(pool, va_h_set, 3 * g + 3)
                pool.tensor_tensor(r2, va_h, half[:, 0:J], ALU.pow).then_inc(r2_set, 1)

            def a_plus_bo(g, par):
                wait_apart(pool, an_set, g + 1)
                pool.tensor_tensor(a[par][:, :, :], a[par][:, :, :],
                                   row[:, 1, :].unsqueeze(1).to_broadcast([P, J, D]), ALU.add).then_inc(abo_set, 1)

            gather(0)
            head(0, 0)
            head_roots(0, 0)
            a_plus_bo(0, 0)

            def step(s, par, first, second, ahead, seq):
                p = s - 1
                if ahead:
                    gather(s + 1)
                if second:
                    wait_apart(pool, wo_taken, 2 * s)
                    wait_apart(pool, out_done, 16 * p)
                    wait_apart(pool, xt_set, p)
                    pool.tensor_tensor(hf[:, :, :], hres[1 - par][:, :, :], a[1 - par][:, :, :], ALU.add).then_inc(hx_add, 1)
                    wait_apart(pool, hx_add, s)
                    pool.tensor_tensor(hf[:, :, :], hf[:, :, :], row[:, 2, :].unsqueeze(1).to_broadcast([P, J, D]),
                                       ALU.add).then_inc(hx_set, 1)
                if ahead:
                    head(s + 1, 1 - par)
                    head_roots(s + 1, 1 - par)
                if first:
                    for n in range(2):
                        if n == 1 and ahead:
                            a_plus_bo(s + 1, 1 - par)
                        wait_apart(pool, gvar_set, 2 * s + n + 1)
                        gv = gvar[:, 32 * n:32 * n + 32]
                        pool.tensor_scalar(gv, gv, 1.0 / HD, EPS, ALU.mult, ALU.add).then_inc(gve_set, 1)
                        wait_apart(pool, gve_set, 2 * s + n + 1)
                        pool.tensor_tensor(grst[:, 32 * n:32 * n + 32], gv, half[:, 0:32], ALU.pow).then_inc(grst_set, 1)
                if second:
                    wait_apart(pool, stats_3, s)
                    pool.tensor_scalar(ve_3, mv_3[:, :, 1], EPS, None, ALU.add).then_inc(ve_3_set, 1)
                    wait_apart(pool, ve_3_set, s)
                    pool.tensor_tensor(r_3, ve_3, half[:, 0:J], ALU.pow).then_inc(r_3_set, 1)
                    wait_apart(pool, dl_set, s)
                    pool.tensor_tensor(ed, euler[:, :], dl, ALU.pow).then_inc(ed_set, 1)
                if first:
                    wait_apart(pool, stats_2, s + 1)
                    pool.tensor_scalar(ve_2, mv_2[:, :, 1], EPS, None, ALU.add).then_inc(ve_2_set, 1)
                    wait_apart(pool, ve_2_set, s + 1)
                    pool.tensor_tensor(r_2, ve_2, half[:, 0:J], ALU.pow).then_inc(r_2_set, 1)
                if second:
                    if isinstance(s, int) and s == 1:
                        pass
                    pool.wait_ge(slots_empty, 16)
                    wait_apart(pool, slot_set, s)
                    wait_apart(pool, wt_set, s)
                    for j in range(J):
                        for k in range(2):
                            pool.indirect_dma_start(
                                xe, bass.IndirectOffsetOnAxis(ap=slot[:, 2 * j + k:2 * j + k + 1], axis=0),
                                pl[:, j, k, :], None, bounds_check=E * CP - 1, oob_is_err=False).then_inc(scattered, 16)
            steps(pool, step)

            def part(e, b, first, last, n):
                if first:
                    pool.wait_ge(out_done, 16 * (G + 1))
                wait_apart(pool, added, 16 * SJ * e)
                for j in range(SJ):
                    if j == 0:
                        wait_apart(pool, yt_taken, 2 * (e + 1))
                    pool.indirect_dma_start(
                        out, bass.IndirectOffsetOnAxis(ap=xr[b][:, j, D:D + 1].bitcast(i32), axis=0),
                        yw[:, j, :], None, compute_op=ALU.add).then_inc(added, 16)
            experts(pool, part)
            pool.wait_ge(added, 16 * SJ * E)

        @block.scalar
        def _(act):
            act.wait_ge(in_small, 16 * 5)

            def vcol(n):
                return vec[:, n:n + 1]

            def normed(g, par):
                wait(act, a_set, g + 1)
                wait(act, r2_set, g + 1)
                for j in range(J):
                    last = act.activation(an[:, j, :], a[par][:, j, :], ACT.Copy, scale=r2[:, j:j + 1])
                last.then_inc(an_set, 1)

            def xT(g):
                for k in range(KD):
                    wait(act, xT_full, KD * g + k + 1)
                    act.activation(xnT[:, k, :], bank[6 + k][:, :], ACT.Identity,
                                   scale=vcol(V_N1W + k), bias=vcol(V_N1B + k)).then_inc(xT_taken, 1)

            normed(0, 0)
            xT(0)

            def step(s, par, first, second, ahead, seq):
                p = s - 1

                def u(j):
                    if not second:
                        return
                    wait(act, u_full, NH * p + j + 1)
                    wait(act, prod_set, NH * p + max(j - 1, 0))
                    w = HW[j]
                    act.activation(su[0:w, j % 2, :], bank[4][0:w, :], ACT.Silu,
                                   bias=vec[0:w, V_BU + j:V_BU + j + 1]).then_inc(u_taken, 1)

                def take_ret(c):
                    if not first:
                        return
                    wait(act, ret_full, J * s + c + 1)
                    if c == 0:
                        wait(act, gn_set, 2 * s)
                    act.activation(ret[:, c, :], bank[6][:, 0:D], ACT.Copy).then_inc(ret_taken, 1)

                def squares(n):
                    if not first:
                        return
                    wait(act, xc_set, 2 * s + n + 1)
                    wait(act, gvar_set, 2 * s + n)
                    act.activation(sq[:, :, :], ret[:, 2 * n:2 * n + 2, :], ACT.Square).then_inc(sq_set, 1)

                if second:
                    for k in range(KD):
                        wait(act, x2T_full, KD * p + k + 1)
                        act.activation(x2T[:, k, :], bank[6 + k][:, :], ACT.Identity,
                                       scale=vcol(V_N2W + k), bias=vcol(V_N2B + k)).then_inc(x2T_taken, 1)
                if first:
                    wait(act, qk_taken, 4 * s + 4)
                    for o in range(2):
                        act.activation(kX[:, o, :, :], kT[:, :, :], ACT.Copy,
                                       scale=const[:, K_PAR + o:K_PAR + o + 1]).then_inc(kX_set, 1)
                    wait(act, gg_set, 2 * s)
                    for m in range(KD):
                        wait(act, gate_full, KD * s + m + 1)
                        act.activation(gateT[:, m, :], bank[4 + m][:, :], ACT.Silu, bias=vcol(V_BG + m)).then_inc(gate_taken, 1)
                    for i in range(2):
                        wait(act, kt_full, 2 * s + i + 1)
                        act.activation(ktok[:, 2 * i:2 * i + 2, :],
                                       bank[2 + i][:, :].rearrange("p (j d) -> p j d", j=2), ACT.Copy).then_inc(kt_taken, 1)
                u(0)
                u(1)
                take_ret(0)
                u(2)
                take_ret(1)
                u(3)
                squares(0)
                take_ret(2)
                u(4)
                take_ret(3)
                if ahead:
                    normed(s + 1, 1 - par)
                u(5)
                squares(1)
                if first:
                    for m in range(KD):
                        wait(act, gnT_full, KD * s + m + 1)
                        act.activation(gnT[:, m, :], bank[m][:, :], ACT.Identity,
                                       scale=vcol(V_GNW + m), bias=vcol(V_GNB + m)).then_inc(gnT_taken, 1)
                if second:
                    for k in range(KD):
                        wait(act, xtT_full, KD * p + k + 1)
                        act.activation(xtT[:, k, :], bank[4 + k][:, :], ACT.Copy).then_inc(xtT_taken, 1)
                if ahead:
                    xT(s + 1)
            steps(act, step)

            act.wait_ge(in_moe, 32)

            def part(e, b, first, last, n):
                def take_x(e, b):
                    for k in range(KD):
                        wait(act, xeT_full, KD * e + k + 1)
                        act.activation(xeT[b][:, k, :], bank[4 + k][:, 0:CP], ACT.Copy).then_inc(xeT_taken, 1)
                if first:
                    take_x(0, 0)
                for m in range(MF):
                    wait(act, h1_full, MF * e + m + 1)
                    if m == 0:
                        wait(act, y_full, KD * e)
                    act.activation(heT[:, m, :], bank[m % 2][:, 0:CP], ACT.Gelu,
                                   bias=B1_e(act, e, m)).then_inc(h1_taken, 1)
                if not last:
                    take_x(e + 1, 1 - b)

            def B1_e(act, e, m):
                return B1[:, :, :].rearrange("p e m -> p (e m)")[:, bass.ds(e * MF + m, 1)]
            experts(act, part)

        @block.vector
        def _(dve):
            dve.wait_ge(in_small, 16 * 5)
            dve.tensor_copy(strict[:, :], const[:, K_STRICT:K_IOTA]).then_inc(strict_set, 1)
            dve.tensor_copy(tokf[:, :], tok0).then_inc(strict_set, 1)
            dve.wait_ge(consts_set, 4)

            def stats(x, st, mv, done, n_bn):
                for j in range(J):
                    last = dve.bn_stats(st[:, j, :], x[:, j, :])
                last.then_inc(bn, 1)
                wait_apart(dve, bn, n_bn)
                for j in range(J):
                    last = dve.bn_aggr(mv[:, j, :], st[:, j, :])
                last.then_inc(done, 1)

            def bn_count(s, first, second, ahead, which):
                n = 1 + (3 * s - 1 if not (isinstance(s, int) and s == 0) else 0)
                if isinstance(s, int) and s == G:
                    n = 1 + 3 * s - 2
                order = [ahead, second, first]
                return n + sum(order[:which + 1])

            def head_stats(g, par, n_bn):
                wait(dve, h_set, g + 1)
                stats(hres[par], st_h, mv_h, stats_h, n_bn)

            def head_norm(g, par):
                wait(dve, r1_set, g + 1)
                wait(dve, hx_add, g - 1)
                for j in range(J):
                    last = dve.tensor_scalar(a[par][:, j, :], hres[par][:, j, :], mv_h[:, j, 0:1], r1[:, j:j + 1],
                                             ALU.subtract, ALU.mult)
                last.then_inc(a_set, 1)

            head_stats(0, 0, 1)
            head_norm(0, 0)

            def step(s, par, first, second, ahead, seq):
                p = s - 1

                def glu(j):
                    if not second:
                        return
                    w = HW[j]
                    wait(dve, g_full, NH * p + j + 1)
                    wait(dve, u_taken, NH * p + j + 1)
                    dve.scalar_tensor_tensor(prodT[0:w, j, :], bank[5][0:w, :], vec[0:w, V_BGL + j:V_BGL + j + 1],
                                             su[0:w, j % 2, :], ALU.add, ALU.mult).then_inc(prod_set, 1)

                def mask(c):
                    if not first:
                        return
                    for q in range(4):
                        wait(dve, sc_full, 16 * s + 4 * c + q + 1)
                        dve.tensor_tensor(sm[:, q, :, :], bank[q][:, :].rearrange("p (h n) -> p h n", h=4),
                                          causal.unsqueeze(1).to_broadcast([P, 4, P]), ALU.mult).then_inc(sc_masked, 1)

                def next_state(c):
                    if not first:
                        return
                    wait(dve, kv_full, J * s + c + 1)
                    if par == 0 and c == 0:
                        dve.tensor_tensor(state[:, :], bank[7][:, 0:D], bd_tab, ALU.mult).then_inc(state_set, 1)
                        return
                    dve.tensor_tensor(stmp[:, :], bank[7][:, 0:D], state[:, :], ALU.add).then_inc(kv_added, 1)
                    dve.wait_ge(kv_added, seq * 7 + (4 * par + c))
                    dve.tensor_tensor(state[:, :], stmp[:, :], bd_tab, ALU.mult).then_inc(state_set, 1)

                def gn_mean(n):
                    if not first:
                        return
                    r4 = ret[:, 2 * n:2 * n + 2, :].rearrange("p j (h d) -> p (j h) d", h=H)
                    gs = gsum[:, 32 * n:32 * n + 32]
                    wait(dve, ret_taken, J * s + 2 * n + 2)
                    dve.tensor_reduce(gs, r4, AX.X, ALU.add).then_inc(gsum_set, 1)
                    wait(dve, gsum_set, 2 * s + n + 1)
                    dve.scalar_tensor_tensor(r4, gs.unsqueeze(2).to_broadcast([P, 32, HD]), -1.0 / HD, r4,
                                             ALU.mult, ALU.add).then_inc(xc_set, 1)

                def gn_var(n):
                    if not first:
                        return
                    wait(dve, sq_set, 2 * s + n + 1)
                    if n == 0:
                        wait(dve, grst_set, 2 * s)
                    dve.tensor_reduce(gvar[:, 32 * n:32 * n + 32],
                                      sq[:, :, :].rearrange("p j (h d) -> p (j h) d", h=H), AX.X, ALU.add).then_inc(gvar_set, 1)

                if first:
                    for n in range(4):
                        w, m = n // 2, n % 2
                        wait(dve, qk_full, 4 * s + n + 1)
                        dve.scalar_tensor_tensor(
                            (qT, kT)[w][:, m, :].rearrange("p (j n) -> p j n", j=J),
                            bank[n][:, :].rearrange("p (j n) -> p j n", j=J),
                            vec[:, (V_BQ, V_BK)[w] + m:(V_BQ, V_BK)[w] + m + 1],
                            (q_tab, k_tab)[w][:, m, :].unsqueeze(1).to_broadcast([P, J, P]),
                            ALU.add, ALU.mult).then_inc(qk_taken, 1)
                    for i in range(2):
                        wait(dve, v_full, 2 * s + i + 1)
                        dve.tensor_tensor(v[:, 2 * i:2 * i + 2, :], bank[i][:, :].rearrange("p (j d) -> p j d", j=2),
                                          row[:, 0, :].unsqueeze(1).to_broadcast([P, 2, D]), ALU.add).then_inc(v_taken, 1)
                glu(0)
                mask(0)
                glu(1)
                if ahead:
                    head_stats(s + 1, 1 - par, bn_count(s, first, second, ahead, 0))
                next_state(0)
                mask(1)
                glu(2)
                next_state(1)
                mask(2)
                glu(3)
                gn_mean(0)
                next_state(2)
                mask(3)
                glu(4)
                gn_var(0)
                next_state(3)
                if ahead:
                    head_norm(s + 1, 1 - par)
                glu(5)
                gn_mean(1)
                gn_var(1)
                if second:
                    wait(dve, hx_set, s)
                    for i in range(2):
                        wait(dve, o_full, 2 * p + i + 1)
                        dve.tensor_tensor(hf[:, 2 * i:2 * i + 2, :], bank[4 + i][:, :].rearrange("p (j d) -> p j d", j=2),
                                          hf[:, 2 * i:2 * i + 2, :], ALU.add).then_inc(hf_set, 1)
                    dve.wait_ge(hf_set, 2 * s)
                    stats(hf, st_3, mv_3, stats_3, bn_count(s, first, second, ahead, 1))
                if first:
                    for n in range(2):
                        wait(dve, grst_set, 2 * s + n + 1)
                        dve.tensor_tensor(gn[:, 2 * n:2 * n + 2, :].rearrange("p j (h d) -> p (j h) d", h=H),
                                          ret[:, 2 * n:2 * n + 2, :].rearrange("p j (h d) -> p (j h) d", h=H),
                                          grst[:, 32 * n:32 * n + 32].unsqueeze(2).to_broadcast([P, 32, HD]),
                                          ALU.mult).then_inc(gn_set, 1)
                if second:
                    wait(dve, r_3_set, s)
                    wait(dve, scattered, 16 * 2 * J * p)
                    for j in range(J):
                        last = dve.tensor_scalar(pl[:, j, :, 0:D], hf[:, j, :].unsqueeze(1).to_broadcast([P, 2, D]),
                                                 mv_3[:, j, 0:1], r_3[:, j:j + 1], ALU.subtract, ALU.mult)
                    last.then_inc(xt_set, 1)
                if first:
                    for m in range(KD):
                        wait(dve, gnT_taken, KD * s + m + 1)
                        dve.tensor_tensor(gnT[:, m, :], gnT[:, m, :], gateT[:, m, :], ALU.mult).then_inc(gg_set, 1)

                def residual(i):
                    if not first:
                        return
                    wait(dve, abo_set, s + 1)
                    wait(dve, wo_full, 2 * s + i + 1)
                    dve.tensor_tensor(a[par][:, 2 * i:2 * i + 2, :], bank[2 + i][:, :].rearrange("p (j d) -> p j d", j=2),
                                      a[par][:, 2 * i:2 * i + 2, :], ALU.add).then_inc(wo_taken, 1)
                residual(0)
                if second:
                    wait(dve, lg_full, s)
                    dve.tensor_tensor(lgs[:, :, :], bank[4][:, 0:J * E].rearrange("p (j e) -> p j e", j=J),
                                      gb[:, :].unsqueeze(1).to_broadcast([P, J, E]), ALU.add).then_inc(lg_taken, 1)
                    wait_apart(dve, lg_taken, s)
                    for j in range(J):
                        last = dve.max(m8[:, j, :], lgs[:, j, :])
                    last.then_inc(top_set, 1)
                    wait(dve, top_set, 2 * p + 1)
                    dve.tensor_tensor(dl, m8[:, :, 1], m8[:, :, 0], ALU.subtract).then_inc(dl_set, 1)
                    for j in range(J):
                        last = dve.max_index(i8[:, j, :], m8[:, j, :], lgs[:, j, :])
                    last.then_inc(top_set, 1)
                    wait(dve, top_set, 2 * p + 2)
                    dve.tensor_copy(idf[:, :, :], i8[:, :, 0:2]).then_inc(route, 1)
                    dve.wait_ge(route, 7 * p + 1)
                    dve.tensor_tensor(oh[:, :, :], iota.unsqueeze(1).to_broadcast([P, J * 2, E]),
                                      idf[:, :, :].rearrange("p j k -> p (j k)").unsqueeze(2).to_broadcast([P, J * 2, E]),
                                      ALU.is_equal).then_inc(oh_set, 1)
                    wait(dve, oh_set, s)
                    o4 = oh[:, :, :].rearrange("p (j k) e -> p j k e", k=2)
                    dve.tensor_tensor(osum[:, :, :], o4[:, :, 0, :], o4[:, :, 1, :], ALU.add).then_inc(osum_set, 1)
                residual(1)
                if first:
                    wait(dve, wo_taken, 2 * s + 2)
                    stats(a[par], st_2, mv_2, stats_2, bn_count(s, first, second, ahead, 2))
                if second:
                    wait(dve, ed_set, s)
                    dve.tensor_scalar(den, ed, 1.0, None, ALU.add).then_inc(route, 1)
                    dve.wait_ge(route, 7 * p + 2)
                    dve.reciprocal(wt1, den).then_inc(route, 1)
                    dve.wait_ge(route, 7 * p + 3)
                    dve.tensor_copy(pl[:, :, 0, D + 1], wt1)
                    dve.tensor_tensor(pl[:, :, 1, D + 1], ed, wt1, ALU.mult)
                    dve.tensor_copy(pl[:, :, :, D].bitcast(i32), tokf[:, :].rearrange("p (j k) -> p j k", k=2)).then_inc(wt_set, 1)
                    wait(dve, wt_set, s)
                    dve.tensor_scalar(tokf[:, :], tokf[:, :], float(GT), None, ALU.add)
                    wait(dve, cnt_full, s)
                    dve.tensor_tensor(ohc[:, :, :].rearrange("p (j k) e -> p j k e", k=2),
                                      bank[5][:, 0:J * E].rearrange("p (j e) -> p j e", j=J).unsqueeze(2).to_broadcast([P, J, 2, E]),
                                      oh[:, :, :].rearrange("p (j k) e -> p j k e", k=2), ALU.mult).then_inc(cnt_taken, 1)
                    dve.tensor_reduce(osg[:, :], osum[:, :, :].rearrange("p j e -> p e j"), AX.X, ALU.add).then_inc(route, 1)
                    dve.wait_ge(cnt_taken, s)
                    dve.tensor_reduce(pos, ohc[:, :, :], AX.X, ALU.add).then_inc(route, 1)
                    dve.wait_ge(route, 7 * p + 5)
                    dve.tensor_tensor(oacc[:, :], oacc[:, :], osg[:, :], ALU.add).then_inc(oacc_set, 1)
                    dve.scalar_tensor_tensor(slf, idf[:, :, :].rearrange("p j k -> p (j k)"), float(CP), pos,
                                             ALU.mult, ALU.add).then_inc(route, 1)
                    dve.tensor_scalar(over, pos, float(C), 1e6, ALU.is_ge, ALU.mult).then_inc(route, 1)
                    dve.wait_ge(route, 7 * p + 7)
                    dve.tensor_tensor(slot[:, :], slf, over, ALU.add).then_inc(slot_set, 1)
                if first:
                    wait(dve, r_2_set, s + 1)
                    for j in range(J):
                        last = dve.tensor_scalar(x2n[:, j, :], a[par][:, j, :], mv_2[:, j, 0:1], r_2[:, j:j + 1],
                                                 ALU.subtract, ALU.mult)
                    last.then_inc(x2n_set, 1)

            steps(dve, step)

            def part(e, b, first, last, n):
                def weighted(e, b):
                    wait(dve, added, 16 * SJ * e)
                    for n in range(2):
                        wait(dve, yt_full, 2 * e + n + 1)
                        for j in ((0, 1), (2,))[n]:
                            ins = dve.tensor_scalar(yw[:, j, :], bank[2 + n][0:SP_, (j % 2) * D:(j % 2 + 1) * D],
                                                    xr[b][:, j, D + 1:D + 2], None, ALU.mult)
                        ins.then_inc(yt_taken, 1)
                if not first:
                    weighted(e - 1, 1 - b)
                for k in range(KD):
                    wait(dve, y_full, KD * e + k + 1)
                    dve.tensor_scalar(yT[:, k, :], bank[6 + k][:, 0:CP],
                                      B2[:, :, :].rearrange("p e k -> p (e k)")[:, bass.ds(e * KD + k, 1)], None,
                                      ALU.add).then_inc(y_taken, 1)
                if last:
                    weighted(e, b)
            dve.wait_ge(in_moe, 32)
            experts(dve, part)

        @block.tensor
        def _(pe):
            pe.wait_ge(in_small, 16 * 5)
            pe.wait_ge(strict_set, 2)
            pe.wait_ge(consts_set, 4)

            def mm(o, l, r, start, stop, loose=False):
                return pe.matmul(o, l, r, start=start, stop=stop, skip_group_check=loose)

            def xT(g):
                wait(pe, an_set, g + 1)
                wait(pe, ret_taken, J * g)
                wait(pe, state_set, J * g)
                for k in range(KD):
                    for j in range(J):
                        last = pe.transpose(bank[6 + k][:, j * P:(j + 1) * P], an[:, j, k * P:(k + 1) * P], ident)
                    last.then_inc(xT_full, 1)

            xT(0)
            pe.wait_ge(in_w, 16 * 5)

            def step(s, par, first, second, ahead, seq):
                p = s - 1

                def glu(j):
                    if not second:
                        return
                    w = HW[j]
                    if j == 0:
                        wait(pe, x2T_taken, KD * s)
                        if first:
                            wait(pe, gate_taken, KD * (s + 1))
                        else:
                            wait(pe, lg_taken, p)
                            wait(pe, cnt_taken, p)
                    wait(pe, u_taken, NH * p + j)
                    for k in range(KD):
                        last = mm(bank[4][0:w, :], Win[:, k, j * P:j * P + w], x2T[:, k, :], k == 0, k == KD - 1)
                    last.then_inc(u_full, 1)
                    wait(pe, prod_set, NH * p + j)
                    for k in range(KD):
                        last = mm(bank[5][0:w, :], Win[:, k, HID + j * P:HID + j * P + w], x2T[:, k, :], k == 0, k == KD - 1)
                    last.then_inc(g_full, 1)

                def score(c, q):
                    if c == 0:
                        if q < 2:
                            wait(pe, v_taken, 2 * s + q + 1)
                        else:
                            wait(pe, kt_taken, 2 * s + q - 1)
                    else:
                        wait(pe, sc_masked, 16 * s + 4 * (c - 1) + q + 1)
                    rows_ = slice(32 * q, 32 * q + 32)
                    t = slice(c * P, (c + 1) * P)
                    for m in range(KD):
                        for o in range(2):
                            n = 2 * m + o
                            last = mm(bank[q][:, n * P:(n + 1) * P], kX[rows_, o, m, t], qT[rows_, m, t], True, True)
                    last.then_inc(sc_full, 1)

                def chunk(c):
                    t = slice(c * P, (c + 1) * P)
                    empty_state = par == 0 and c == 0
                    if c > 0:
                        wait(pe, ret_taken, J * s + c)
                    if not empty_state:
                        wait(pe, state_set, J * s + c)
                        for m in range(KD):
                            mm(bank[6][:, m * P:(m + 1) * P], qT[:, m, t], state[:, m * P:(m + 1) * P], m == 0, False, True)
                    for m in range(KD):
                        last = mm(bank[7][:, m * P:(m + 1) * P], ktok[:, c, m * P:(m + 1) * P], v[:, c, m * P:(m + 1) * P],
                                  True, True)
                    last.then_inc(kv_full, 1)
                    for q in range(4):
                        wait(pe, sc_masked, 16 * s + 4 * c + q + 1)
                        for n in range(4):
                            h = (n // 2) * 8 + 2 * q + n % 2
                            last = mm(bank[6][:, h * HD:(h + 1) * HD], sm[:, q, n, :], v[:, c, h * HD:(h + 1) * HD],
                                      empty_state and q == 0 and n == 0, q == 3 and n == 3, True)
                        if q == 3:
                            last.then_inc(ret_full, 1)
                        if c < J - 1:
                            score(c + 1, q)

                if first:
                    wait(pe, xT_taken, KD * (s + 1))
                    for n in range(4):
                        W, m = (Wq, Wk)[n // 2], n % 2
                        if n == 0:
                            wait(pe, gnT_taken, KD * s)
                        if n == 2:
                            wait(pe, wo_taken, 2 * s)
                        for k in range(KD):
                            last = mm(bank[n][:, :], W[:, k, m * P:(m + 1) * P], xnT[:, k, :], k == 0, k == KD - 1)
                        last.then_inc(qk_full, 1)
                if second:
                    wait(pe, x2n_set, s)
                    for k in range(KD):
                        for j in range(J):
                            last = pe.transpose(bank[6 + k][:, j * P:(j + 1) * P], x2n[:, j, k * P:(k + 1) * P], ident)
                        last.then_inc(x2T_full, 1)
                if first:
                    wait(pe, lg_taken, p)
                    wait(pe, cnt_taken, p)
                    for m in range(KD):
                        for k in range(KD):
                            last = mm(bank[4 + m][:, :], Wg[:, k, m * P:(m + 1) * P], xnT[:, k, :], k == 0, k == KD - 1)
                        last.then_inc(gate_full, 1)
                    for i in range(2):
                        wait(pe, qk_taken, 4 * s + i + 1)
                        for jj in range(2):
                            j = 2 * i + jj
                            for k in range(KD):
                                last = mm(bank[i][:, jj * D:(jj + 1) * D], xnT[:, k, j * P:(j + 1) * P], Wv[:, k, :],
                                          k == 0, k == KD - 1)
                        last.then_inc(v_full, 1)
                    wait(pe, qk_taken, 4 * s + 4)
                    for i in range(2):
                        for jj in range(2):
                            j = 2 * i + jj
                            for m in range(KD):
                                last = pe.transpose(bank[2 + i][:, jj * D + m * P:jj * D + (m + 1) * P],
                                                    kT[:, m, j * P:(j + 1) * P], ident)
                        last.then_inc(kt_full, 1)
                if second and isinstance(s, int) and s == 1 or not isinstance(s, int):
                    pe.wait_ge(in_ffn, 48)
                glu(0)
                if first:
                    wait(pe, kX_set, 2 * (s + 1))
                    for q in range(4):
                        score(0, q)
                    if second:
                        wait(pe, x2T_taken, KD * s)
                    wait(pe, kt_taken, 2 * (s + 1))
                    wait(pe, v_taken, 2 * (s + 1))
                for c in range(J):
                    glu(c + 1)
                    if first:
                        chunk(c)
                glu(NH - 1)
                if second:
                    wait(pe, prod_set, NH * s)
                    for i in range(2):
                        for jj in range(2):
                            j = 2 * i + jj
                            for n in range(NH):
                                w = HW[n]
                                last = mm(bank[4 + i][:, jj * D:(jj + 1) * D], prodT[0:w, n, j * P:(j + 1) * P],
                                          Wout[0:w, n, :], n == 0, n == NH - 1)
                        last.then_inc(o_full, 1)
                if first:
                    wait(pe, gn_set, 2 * (s + 1))
                    wait(pe, sc_masked, 16 * (s + 1))
                    for m in range(KD):
                        for j in range(J):
                            last = pe.transpose(bank[m][:, j * P:(j + 1) * P], gn[:, j, m * P:(m + 1) * P], ident)
                        last.then_inc(gnT_full, 1)
                if second:
                    wait(pe, xt_set, s)
                    wait(pe, hf_set, 2 * s)
                    for k in range(KD):
                        for j in range(J):
                            last = pe.transpose(bank[4 + k][:, j * P:(j + 1) * P], pl[:, j, 0, k * P:(k + 1) * P], ident)
                        last.then_inc(xtT_full, 1)
                if ahead:
                    xT(s + 1)

                def out_proj(i):
                    if not first:
                        return
                    wait(pe, gg_set, KD * (s + 1))
                    for jj in range(2):
                        j = 2 * i + jj
                        for m in range(KD):
                            last = mm(bank[2 + i][:, jj * D:(jj + 1) * D], gnT[:, m, j * P:(j + 1) * P], Wo[:, m, :],
                                      m == 0, m == KD - 1)
                    last.then_inc(wo_full, 1)
                out_proj(0)
                if second:
                    wait(pe, xtT_taken, KD * s)
                    for j in range(J):
                        for k in range(KD):
                            last = mm(bank[4][:, j * E:(j + 1) * E], xtT[:, k, j * P:(j + 1) * P], Gw[:, k, :], k == 0, k == KD - 1)
                    last.then_inc(lg_full, 1)
                out_proj(1)
                if second:
                    wait(pe, osum_set, s)
                    wait(pe, oacc_set, p)
                    for j in range(J):
                        o = bank[5][:, j * E:(j + 1) * E]
                        mm(o, strict[:, :], osum[:, j, :], True, False)
                        for i in range(j):
                            mm(o, ones[:, :], osum[:, i, :], False, False)
                        last = mm(o, ones[:, :], oacc[:, :], False, True)
                    last.then_inc(cnt_full, 1)

            def chunk(c):
                chunk(c).then_inc(ret_full, 1)
            steps(pe, step)

            def part(e, b, first, last, n):
                def to_features(e, b, n):
                    wait(pe, xr_in[b], 16 * n)
                    wait(pe, xeT_taken, KD * e)
                    for k in range(KD):
                        for j in range(SJ):
                            ins = pe.transpose(bank[4 + k][:, j * SP_:(j + 1) * SP_], xr[b][:, j, k * P:(k + 1) * P],
                                               const[0:SP_, K_ID:K_ID + SP_])
                        ins.then_inc(xeT_full, 1)

                def to_tokens(e):
                    wait(pe, y_taken, KD * (e + 1))
                    wait(pe, yt_taken, 2 * e)
                    for n in range(2):
                        for j in ((0, 1), (2,))[n]:
                            for k in range(KD):
                                ins = pe.transpose(bank[2 + n][0:SP_, (j % 2) * D + k * P:(j % 2) * D + (k + 1) * P],
                                                   yT[:, k, j * SP_:(j + 1) * SP_], ident)
                        ins.then_inc(yt_full, 1)

                if first:
                    to_features(0, 0, 1)
                wait(pe, w1_in[b], 16 * n)
                wait(pe, xeT_taken, KD * (e + 1))
                for m in range(MF):
                    wait(pe, h1_taken, MF * e + m - 1)
                    for k in range(KD):
                        ins = mm(bank[m % 2][:, 0:CP], W1[b][:, k, m * P:(m + 1) * P], xeT[b][:, k, :], k == 0, k == KD - 1)
                    ins.then_inc(h1_full, 1)
                if not first:
                    to_tokens(e - 1)
                if not last:
                    to_features(e + 1, 1 - b, n if b == 0 else n + 1)
                wait(pe, w2_in[b], 16 * n)
                wait(pe, h1_taken, MF * (e + 1))
                for k in range(KD):
                    wait(pe, y_taken, KD * e)
                    for m in range(MF):
                        ins = mm(bank[6 + k][:, 0:CP], W2[b][:, m, k * P:(k + 1) * P], heT[:, m, :], m == 0, m == MF - 1)
                    ins.then_inc(y_full, 1)
                if last:
                    to_tokens(e)

            experts(pe, part)


def kernel(**x):
    import concourse.bacc as _bacc
    from concourse.bass_utils import run_bass_kernel_spmd as _run

    def get(name):
        return np.asarray(x[name])

    def columns(a, n):
        a = np.concatenate([a, np.zeros(n * P - a.shape[0], a.dtype)])
        return a.reshape(n, P).T

    A, M = "L0_attn_", "L0_ffn_"
    consts, empty = shape_constants()
    b_in = get(A + "b_in")
    vecs = np.concatenate(
        [columns(get(A + n), KD) for n in ("norm1_w", "norm1_b", "bq", "bk", "bg", "gn_w", "gn_b", "norm2_w", "norm2_b")]
        + [columns(b_in[:HID], NH), columns(b_in[HID:], NH)], axis=1)
    arrays = {
        "idx": get("x").reshape(G, J, P).transpose(0, 2, 1),
        "emb": get("L0_tok_emb_table"),
        "consts": consts, "empty": empty, "vecs": vecs,
        "rows": np.stack([get(A + n) for n in ("bv", "bo", "b_out")]),
        **{n: get(A + n) for n in ("wq", "wk", "wv", "wg", "wo", "w_in", "w_out")},
        "gate_w": get(M + "gate_w"), "gate_b": get(M + "gate_b"),
        "w1": get(M + "w1").reshape(E, KD, P, F).transpose(0, 2, 1, 3),
        "b1": get(M + "b1").reshape(E, MF, P).transpose(2, 0, 1),
        "w2": get(M + "w2").reshape(E, MF, P, D).transpose(0, 2, 1, 3),
        "b2": get(M + "b2").reshape(E, KD, P).transpose(2, 0, 1),
    }
    arrays = {n: np.ascontiguousarray(v) for n, v in arrays.items()}
    nc = _bacc.Bacc("TRN2", target_bir_lowering=False, num_devices=1)
    args = [nc.dram_tensor(n, v.shape, mybir.dt.from_np(v.dtype), kind="ExternalInput").ap() for n, v in arrays.items()]
    out = nc.dram_tensor("out", [T + DUMP, D], f32, kind="ExternalOutput").ap()
    xe = nc.dram_tensor("xe", [E * CP, ROW], f32, kind="Internal").ap()
    build(nc, *args, out, xe)
    r = _run(nc, [arrays], core_ids=[0])
    return r.results[0]["out"][:T].reshape(B, S, D)
```

```python
import concourse.bass as bass
from concourse import mybir
from contextlib import ExitStack
import numpy as np

f32 = mybir.dt.float32
f32r = mybir.dt.float32r
bf16 = mybir.dt.bfloat16
i32 = mybir.dt.int32
u32 = mybir.dt.uint32
ALU = mybir.AluOpType
ACT = mybir.ActivationFunctionType
AX = mybir.AxisListType

P = 128
B, S, D = 4, 1024, 256
T = B * S
KD = D // P
H, HD = 16, 16
J = 4
GT = J * P
G = T // GT
HID = 682
NH = -(-HID // P)
HW = [min(P, HID - n * P) for n in range(NH)]
E, F, C = 32, 1024, 308
MF = F // P
SP_ = 104
SJ = 3
CP = SP_ * SJ
ROW = D + 2
EPS = 1e-5
DUMP = CP

V_N1W, V_N1B, V_BQ, V_BK, V_BG, V_GNW, V_GNB, V_N2W, V_N2B = range(0, 18, 2)
V_BU = 18
V_BGL = V_BU + NH
V_ALL = V_BGL + NH

K_PE = 0
K_Q = K_PE + 8 * D
K_K = K_Q + KD * P
K_BD = K_K + KD * P
K_CAUSAL = K_BD + KD * P
K_ID = K_CAUSAL + P
K_STRICT = K_ID + P
K_IOTA = K_STRICT + P
K_TOK = K_IOTA + E
K_PAR = K_TOK + 8
K_ALL = K_PAR + 4


def shape_constants():
    c = np.zeros((P, K_ALL), np.float32)
    p = np.arange(P)
    pos = np.arange(S, dtype=np.float32)
    inv = np.power(np.float32(10000.0), (np.float32(-2.0) * np.arange(D // 2, dtype=np.float32) / np.float32(D))).astype(np.float32)
    ang = (pos[:, None] * inv[None, :]).astype(np.float32).astype(np.float64)
    pe = np.stack([np.sin(ang), np.cos(ang)], -1).reshape(S, D)
    c[:, K_PE:K_Q] = pe.reshape(8, P, D).transpose(1, 0, 2).reshape(P, -1)
    gamma = 1.0 - 2.0 ** (-5.0 - np.arange(H))
    feature = np.arange(D).reshape(KD, P)
    gf = gamma[feature // HD].T
    c[:, K_Q:K_K] = (HD ** -0.5 * gf[:, :, None] ** p[None, None, :]).reshape(P, -1)
    c[:, K_K:K_BD] = (gf[:, :, None] ** -p[None, None, :].astype(np.float64)).reshape(P, -1)
    same = (p[:, None] // HD == p[None, :] // HD)
    c[:, K_BD:K_CAUSAL] = (gf[:, :, None] ** P * same[:, None, :]).reshape(P, -1)
    c[:, K_CAUSAL:K_ID] = p[:, None] <= p[None, :]
    c[:, K_ID:K_STRICT] = np.eye(P)
    c[:, K_STRICT:K_IOTA] = p[:, None] < p[None, :]
    c[:, K_IOTA:K_TOK] = np.arange(E)[None, :]
    c[:, K_TOK:K_PAR] = (np.arange(J)[None, :, None] * P + p[:, None, None] + np.zeros((1, 1, 2))).reshape(P, -1)
    c[:, K_PAR:K_ALL] = (p[:, None] // HD) % 4 == np.arange(4)
    empty = np.zeros((SP_, SJ, ROW), np.float32)
    empty[:, :, D] = (T + np.arange(CP, dtype=np.int32).reshape(SP_, SJ)).astype(np.int32).view(np.float32)
    return c, empty


def build(nc, idx, emb, consts, empty, vecs, rows, wq, wk, wv, wg, wo, w_in, w_out, gate_w, gate_b, w1, b1, w2, b2,
          out, xe):
    ctx = ExitStack()
    with ctx:
        place = [ctx]

        def sb(name, shape, dt=f32):
            return place[-1].enter_context(nc.sbuf_tensor(name, shape, dt))

        def sem(name):
            return ctx.enter_context(nc.semaphore(name))

        const = sb("const", [P, K_ALL])
        vec = sb("vec", [P, V_ALL])
        row = sb("row", [P, 3, D])
        gb = sb("gb", [P, E])
        B1 = sb("B1", [P, E, MF])
        B2 = sb("B2", [P, E, KD])
        W1 = sb("W1", [P, KD, F])
        W2 = sb("W2", [P, MF, D])

        place.append(ExitStack())
        Wq, Wk, Wv, Wg, Wo = (sb(n, [P, KD, D]) for n in ("Wq", "Wk", "Wv", "Wg", "Wo"))
        Win = sb("Win", [P, KD, 2 * HID])
        Wout = sb("Wout", [P, NH, D])
        Gw = sb("Gw", [P, KD, E])
        strict = sb("strict", [P, P], bf16)
        ones = sb("ones", [P, P], bf16)
        half = sb("half", [P, 64])
        euler = sb("euler", [P, J])

        pe_tab = const[:, K_PE:K_Q].rearrange("p (c d) -> p c d", d=D)
        q_tab = const[:, K_Q:K_K].rearrange("p (m n) -> p m n", m=KD)
        k_tab = const[:, K_K:K_BD].rearrange("p (m n) -> p m n", m=KD)
        bd_tab = const[:, K_BD:K_CAUSAL]
        causal = const[:, K_CAUSAL:K_ID]
        ident = const[:, K_ID:K_STRICT]
        iota = const[:, K_IOTA:K_TOK]
        tok0 = const[:, K_TOK:K_PAR]

        idxg = sb("idxg", [P, J], i32)
        emb_in = sb("emb_in", [P, J, D])
        hres = [sb(f"hres{n}", [P, J, D]) for n in range(2)]
        a = [sb(f"a{n}", [P, J, D]) for n in range(2)]
        an = sb("an", [P, J, D])
        xnT = sb("xnT", [P, KD, GT])
        qT = sb("qT", [P, KD, GT])
        kT = sb("kT", [P, KD, GT])
        kX = sb("kX", [P, 4, KD, GT])
        gateT = sb("gateT", [P, KD, GT])
        vz = sb("vz", [P, J, H * 4 * HD])
        ktok = sb("ktok", [P, J, D])
        sm = sb("sm", [P, J, 4, P])
        state = sb("state", [P, KD * P])
        stmp = sb("stmp", [P, KD * P])
        ret = sb("ret", [P, J, D])
        sq = sb("sq", [P, 2, D])
        gn = sb("gn", [P, J, D])
        gnT = sb("gnT", [P, KD, GT])
        x2n = sb("x2n", [P, J, D])
        x2T = sb("x2T", [P, KD, GT])
        su = sb("su", [P, 2, GT])
        prodT = sb("prodT", [P, NH, GT])
        hf = sb("hf", [P, J, D])
        pl = sb("pl", [P, J, 2, ROW])
        emptyrow = pl[0:SP_, :, :, :].rearrange("p j k n -> p (j k n)")[:, 0:SJ * ROW]
        xtT = sb("xtT", [P, KD, GT])
        lgs = sb("lgs", [P, J, E])
        oh = sb("oh", [P, J * 2, E])
        ohc = sb("ohc", [P, J * 2, E])
        osum = sb("osum", [P, J, E], bf16)
        oacc = sb("oacc", [P, E], bf16)
        osg = sb("osg", [P, E])
        slot = sb("slot", [P, J * 2], i32)
        tokf = sb("tokf", [P, J * 2])
        m8 = sb("m8", [P, J, 8])
        i8 = sb("i8", [P, J, 8], u32)
        idf = sb("idf", [P, J, 2])
        small = sb("small", [P, 360])
        off = [0]

        def tiny(n):
            off[0] += n
            return small[:, off[0] - n:off[0]]

        st_h, st_2, st_3 = (tiny(24).rearrange("p (j n) -> p j n", j=J) for _ in range(3))
        mv_h, mv_2, mv_3 = (tiny(8).rearrange("p (j n) -> p j n", j=J) for _ in range(3))
        ve_h, r1, va_h, r2, ve_2, r_2, ve_3, r_3, dl, ed, den, wt1 = (tiny(J) for _ in range(12))
        gsum, gvar, grst = (tiny(64) for _ in range(3))
        pos, slf, over = (tiny(J * 2) for _ in range(3))

        place.pop().close()
        place.append(ctx.enter_context(ExitStack()))
        W1h, W1l = (sb(n, [P, KD, F], f32r) for n in ("W1h", "W1l"))
        W2h, W2l = (sb(n, [P, MF, D], f32r) for n in ("W2h", "W2l"))
        xr = [sb(f"xr{n}", [SP_, SJ, ROW]) for n in range(2)]
        meta = [sb(f"meta{n}", [SP_, SJ, 2]) for n in range(2)]
        xeh, xel = (sb(n, [P, KD, CP], f32r) for n in ("xeh", "xel"))
        he = sb("he", [P, 2, CP])
        heh, hel = (sb(n, [P, MF, CP], f32r) for n in ("heh", "hel"))
        yT = sb("yT", [P, KD, CP])
        yw = sb("yw", [SP_, SJ, D])

        bank = [ctx.enter_context(nc.psum_tensor(f"bank{n}", [P, 512], f32)) for n in range(8)]

        in_small, in_w, in_ffn, in_moe, in_empty = (sem(n) for n in ("in_small", "in_w", "in_ffn", "in_moe", "in_empty"))
        consts_set = sem("consts_set")
        strict_set = sem("strict_set")
        passed = sem("passed")
        slots_empty = sem("slots_empty")
        first_idx_in, idx_in, emb_landed = sem("first_idx_in"), sem("idx_in"), sem("emb_landed")
        h_set, stats_h, ve_h_set, va_h_set, r1_set, r2_set, a_set, an_set, abo_set = (
            sem(n) for n in ("h_set", "stats_h", "ve_h_set", "va_h_set", "r1_set", "r2_set", "a_set", "an_set", "abo_set"))
        xT_full, xT_taken = sem("xT_full"), sem("xT_taken")
        qk_full, qk_taken = sem("qk_full"), sem("qk_taken")
        gate_full, gate_taken = sem("gate_full"), sem("gate_taken")
        v_full, v_taken = sem("v_full"), sem("v_taken")
        kt_full, kt_taken = sem("kt_full"), sem("kt_taken")
        kX_set = sem("kX_set")
        sc_full, sc_masked = sem("sc_full"), sem("sc_masked")
        kv_full, kv_added, state_set = sem("kv_full"), sem("kv_added"), sem("state_set")
        ret_full, ret_taken = sem("ret_full"), sem("ret_taken")
        gsum_set, xc_set, sq_set, gvar_set, gve_set, grst_set, gn_set = (
            sem(n) for n in ("gsum_set", "xc_set", "sq_set", "gvar_set", "gve_set", "grst_set", "gn_set"))
        gnT_full, gnT_taken, gg_set = sem("gnT_full"), sem("gnT_taken"), sem("gg_set")
        wo_full, wo_taken = sem("wo_full"), sem("wo_taken")
        stats_2, ve_2_set, r_2_set, x2n_set = (sem(n) for n in ("stats_2", "ve_2_set", "r_2_set", "x2n_set"))
        x2T_full, x2T_taken = sem("x2T_full"), sem("x2T_taken")
        u_full, u_taken, g_full, prod_set = sem("u_full"), sem("u_taken"), sem("g_full"), sem("prod_set")
        hx_add, hx_set = sem("hx_add"), sem("hx_set")
        o_full, hf_set, out_done = sem("o_full"), sem("hf_set"), sem("out_done")
        stats_3, ve_3_set, r_3_set, xt_set = (sem(n) for n in ("stats_3", "ve_3_set", "r_3_set", "xt_set"))
        xtT_full, xtT_taken = sem("xtT_full"), sem("xtT_taken")
        lg_full, lg_taken = sem("lg_full"), sem("lg_taken")
        top_set, dl_set, ed_set, oh_set, osum_set = (sem(n) for n in ("top_set", "dl_set", "ed_set", "oh_set", "osum_set"))
        route = sem("route")
        cnt_full, cnt_taken = sem("cnt_full"), sem("cnt_taken")
        oacc_set, slot_set, wt_set = sem("oacc_set"), sem("slot_set"), sem("wt_set")
        scattered = sem("scattered")
        bn, bn_3 = sem("bn"), sem("bn_3")
        w1_in, w2_in = sem("w1_in"), sem("w2_in")
        w1h_set, w1l_set = sem("w1h_set"), sem("w1l_set")
        w2h_set, w2l_set, w2l_also = sem("w2h_set"), sem("w2l_set"), sem("w2l_also")
        meta_set = sem("meta_set")
        heh_set, hel_set = sem("heh_set"), sem("hel_set")
        xr_in = [sem(f"xr_in{n}") for n in range(2)]
        xeT_full, xeh_set, xel_set = sem("xeT_full"), sem("xeh_set"), sem("xel_set")
        h1_full, h1_taken = sem("h1_full"), sem("h1_taken")
        y_full, y_taken = sem("y_full"), sem("y_taken")
        yt_full, yt_taken = sem("yt_full"), sem("yt_taken")
        added = sem("added")

        block = ctx.enter_context(nc.Block())

        def wait(eng, s, n):
            if isinstance(n, int) and n <= 0:
                return
            eng.wait_ge(s, n)

        def wait_apart(eng, s, n):
            wait(eng, s, n)
            if not isinstance(n, int):
                eng.sem_inc(passed, 1)

        def own_columns(j, g, n):
            whole = vz[:, j, g * 256:g * 256 + 16]
            return bass.AP(whole.tensor, whole.offset, [list(whole.ap[0]), [256, n], [4 * HD + HD, 4], [1, HD]])

        def steps(eng, step):
            step(0, 0, True, False, True, 0)
            step(1, 1, True, True, True, 0)
            with eng.Fori(0, (G - 4) // 2) as i:
                for r in range(2):
                    step(i * 2 + (2 + r), r, True, True, True, i + 1)
            step(G - 2, 0, True, True, True, G // 2 - 1)
            step(G - 1, 1, True, True, False, G // 2 - 1)
            step(G, 0, False, True, False, G // 2)

        def experts(eng, part):
            part(0, 0, True, False, 1)
            part(1, 1, False, False, 1)
            with eng.Fori(0, (E - 4) // 2) as i:
                for r in range(2):
                    part(i * 2 + (2 + r), r, False, False, i + 2)
            part(E - 2, 0, False, False, E // 2)
            part(E - 1, 1, False, True, E // 2)

        @block.sync
        def _(sp):
            sp.dma_start(idxg[:, :], idx[0]).then_inc(first_idx_in, 16)
            sp.dma_start(const[:, :], consts).then_inc(in_small, 16)
            sp.dma_start(vec[:, :], vecs).then_inc(in_small, 16)
            sp.dma_start(row[:, :, :], rows.partition_broadcast(P)).then_inc(in_small, 16)
            sp.dma_start(gb[:, :], gate_b.partition_broadcast(P)).then_inc(in_small, 16)
            sp.dma_start(Gw[:, :, :], gate_w.rearrange("(k p) n -> p k n", p=P)).then_inc(in_small, 16)
            for dst, src in ((Wq, wq), (Wk, wk), (Wg, wg), (Wv, wv), (Wo, wo)):
                sp.dma_start(dst[:, :, :], src.rearrange("(k p) n -> p k n", p=P)).then_inc(in_w, 16)
            sp.wait_ge(emb_landed, 16 * J)
            sp.dma_start(Win[:, :, :], w_in.rearrange("(k p) n -> p k n", p=P)).then_inc(in_ffn, 16)
            full = HID // P
            sp.dma_start(Wout[:, 0:full, :], w_out[0:full * P, :].rearrange("(k p) n -> p k n", p=P)).then_inc(in_ffn, 16)
            sp.dma_start(Wout[0:HID - full * P, full, :], w_out[full * P:HID, :]).then_inc(in_ffn, 16)
            sp.dma_start(emptyrow, empty.rearrange("p j n -> p (j n)")).then_inc(in_empty, 16)
            sp.dma_start(B1[:, :, :], b1).then_inc(in_moe, 16)
            sp.dma_start(B2[:, :, :], b2).then_inc(in_moe, 16)
            sp.dma_start(W1[:, :, :], w1[0]).then_inc(w1_in, 16)
            sp.dma_start(W2[:, :, :], w2[0]).then_inc(w2_in, 16)

            sp.wait_ge(emb_landed, 16 * 2 * J)
            sp.wait_ge(in_empty, 16)
            sp.dma_start(xe.rearrange("(e p j) n -> p e (j n)", e=E, p=SP_),
                         emptyrow.unsqueeze(1).to_broadcast([SP_, E, SJ * ROW])).then_inc(slots_empty, 16)
            sp.dma_start(out[T:T + DUMP, :].rearrange("(p j) d -> p (j d)", p=SP_), emptyrow[:, 0:SJ * D]).then_inc(slots_empty, 16)

            out_g = out[0:T, :].rearrange("(g j p) d -> g p j d", j=J, p=P)

            def step(s, par, first, second, ahead, seq):
                if second:
                    wait(sp, hf_set, 2 * s)
                    sp.dma_start(out_g[s - 1], hf[:, :, :]).then_inc(out_done, 16)
            steps(sp, step)

            sp.wait_ge(scattered, 16 * 2 * J * G)
            xe_e = xe.rearrange("(e p j) n -> e p j n", e=E, p=SP_)

            def part(e, b, first, last, n):
                if first:
                    sp.dma_start(xr[0][:, :, :], xe_e[0]).then_inc(xr_in[0], 16)
                if last:
                    return
                if not first:
                    wait(sp, xeT_full, KD * e)
                    wait(sp, meta_set, e)
                sp.dma_start(xr[1 - b][:, :, :], xe_e[e + 1]).then_inc(xr_in[1 - b], 16)
                wait(sp, w1l_set, KD * (e + 1))
                sp.dma_start(W1[:, :, :], w1[e + 1]).then_inc(w1_in, 16)
                wait(sp, w2l_set, e + 1)
                wait(sp, w2l_also, e + 1)
                sp.dma_start(W2[:, :, :], w2[e + 1]).then_inc(w2_in, 16)
            experts(sp, part)
            sp.wait_ge(out_done, 16 * G)

        @block.gpsimd
        def _(pool):
            def gather(g):
                wait_apart(pool, h_set, g)
                if not (isinstance(g, int) and g == 0):
                    pool.dma_start(idxg[:, :], idx[g]).then_inc(idx_in, 16)
                    wait_apart(pool, idx_in, 16 * g)
                else:
                    pool.wait_ge(first_idx_in, 16)
                for j in range(J):
                    pool.indirect_dma_start(emb_in[:, j, :], None, emb,
                                            bass.IndirectOffsetOnAxis(ap=idxg[:, j:j + 1], axis=0)).then_inc(emb_landed, 16)

            def head(g, par):
                wait_apart(pool, emb_landed, 16 * J * (g + 1))
                pool.tensor_tensor(hres[par][:, :, :], emb_in[:, :, :], pe_tab[:, J * par:J * par + J, :],
                                   ALU.add).then_inc(h_set, 1)

            def head_roots(g, par):
                wait_apart(pool, stats_h, g + 1)
                pool.tensor_scalar(ve_h, mv_h[:, :, 1], EPS, None, ALU.add).then_inc(ve_h_set, 1)
                wait_apart(pool, ve_h_set, g + 1)
                pool.tensor_tensor(r1, ve_h, half[:, 0:J], ALU.pow).then_inc(r1_set, 1)
                wait_apart(pool, r1_set, g + 1)
                pool.tensor_tensor(va_h, r1, r1, ALU.mult).then_inc(va_h_set, 1)
                wait_apart(pool, va_h_set, 3 * g + 1)
                pool.tensor_tensor(va_h, va_h, mv_h[:, :, 1], ALU.mult).then_inc(va_h_set, 1)
                wait_apart(pool, va_h_set, 3 * g + 2)
                pool.tensor_scalar(va_h, va_h, EPS, None, ALU.add).then_inc(va_h_set, 1)
                wait_apart(pool, va_h_set, 3 * g + 3)
                pool.tensor_tensor(r2, va_h, half[:, 0:J], ALU.pow).then_inc(r2_set, 1)

            def a_plus_bo(g, par):
                wait_apart(pool, an_set, g + 1)
                pool.tensor_tensor(a[par][:, :, :], a[par][:, :, :],
                                   row[:, 1, :].unsqueeze(1).to_broadcast([P, J, D]), ALU.add).then_inc(abo_set, 1)

            gather(0)
            pool.memset(half[:, :], -0.5).then_inc(consts_set, 1)
            pool.memset(euler[:, :], float(np.e)).then_inc(consts_set, 1)
            pool.memset(ones[:, :], 1.0).then_inc(consts_set, 1)
            pool.memset(oacc[:, :], 0.0).then_inc(consts_set, 1)
            pool.wait_ge(consts_set, 4)
            pool.wait_ge(in_small, 16 * 5)
            head(0, 0)
            head_roots(0, 0)
            gather(1)
            a_plus_bo(0, 0)

            def scatter(s):
                if isinstance(s, int) and s < 2:
                    return
                pool.wait_ge(slots_empty, 32)
                wait_apart(pool, slot_set, s - 1)
                wait_apart(pool, wt_set, s - 1)
                for j in range(J):
                    for k in range(2):
                        pool.indirect_dma_start(
                            xe, bass.IndirectOffsetOnAxis(ap=slot[:, 2 * j + k:2 * j + k + 1], axis=0),
                            pl[:, j, k, :], None, bounds_check=E * CP - 1, oob_is_err=False).then_inc(scattered, 16)

            def step(s, par, first, second, ahead, seq):
                p = s - 1
                if second:
                    wait_apart(pool, wo_taken, 2 * s)
                    wait_apart(pool, out_done, 16 * p)
                    wait_apart(pool, xt_set, 2 * p)
                    pool.tensor_tensor(hf[:, :, :], hres[1 - par][:, :, :], a[1 - par][:, :, :], ALU.add).then_inc(hx_add, 1)
                    wait_apart(pool, hx_add, s)
                    pool.tensor_tensor(hf[:, :, :], hf[:, :, :], row[:, 2, :].unsqueeze(1).to_broadcast([P, J, D]),
                                       ALU.add).then_inc(hx_set, 1)
                scatter(s)
                if ahead:
                    head(s + 1, 1 - par)
                    if not isinstance(s, int) or s + 2 < G:
                        gather(s + 2)
                    head_roots(s + 1, 1 - par)
                if first:
                    for n in range(2):
                        wait_apart(pool, gvar_set, 2 * s + n + 1)
                        gv = gvar[:, 32 * n:32 * n + 32]
                        pool.tensor_scalar(gv, gv, 1.0 / HD, EPS, ALU.mult, ALU.add).then_inc(gve_set, 1)
                        wait_apart(pool, gve_set, 2 * s + n + 1)
                        pool.tensor_tensor(grst[:, 32 * n:32 * n + 32], gv, half[:, 0:32], ALU.pow).then_inc(grst_set, 1)
                if ahead:
                    a_plus_bo(s + 1, 1 - par)
                if second:
                    for i in range(2):
                        v, t = ve_3[:, 2 * i:2 * i + 2], 2 * p + i + 1
                        wait_apart(pool, stats_3, t)
                        pool.tensor_scalar(v, mv_3[:, 2 * i:2 * i + 2, 1], EPS, None, ALU.add).then_inc(ve_3_set, 1)
                        wait_apart(pool, ve_3_set, t)
                        pool.tensor_tensor(r_3[:, 2 * i:2 * i + 2], v, half[:, 0:2], ALU.pow).then_inc(r_3_set, 1)
                    wait_apart(pool, dl_set, s)
                    pool.tensor_tensor(ed, euler[:, :], dl, ALU.pow).then_inc(ed_set, 1)
                if first:
                    wait_apart(pool, stats_2, s + 1)
                    pool.tensor_scalar(ve_2, mv_2[:, :, 1], EPS, None, ALU.add).then_inc(ve_2_set, 1)
                    wait_apart(pool, ve_2_set, s + 1)
                    pool.tensor_tensor(r_2, ve_2, half[:, 0:J], ALU.pow).then_inc(r_2_set, 1)
            steps(pool, step)
            scatter(G + 1)

            def w2_low(e):
                wait_apart(pool, w2h_set, KD * (e + 1))
                t = slice(MF // 2, MF)
                pool.tensor_tensor(W2l[:, t, :], W2[:, t, :], W2h[:, t, :].bitcast(f32), ALU.subtract).then_inc(w2l_also, 1)

            def part(e, b, first, last, n):
                if first:
                    w2_low(0)
                    pool.wait_ge(out_done, 16 * G)
                wait_apart(pool, xr_in[b], 16 * n)
                wait_apart(pool, added, 16 * SJ * e)
                pool.tensor_copy(meta[b][:, :, :], xr[b][:, :, D:ROW]).then_inc(meta_set, 1)
                if not last:
                    w2_low(e + 1)
                wait_apart(pool, meta_set, e + 1)
                wait_apart(pool, yt_taken, SJ * (e + 1))
                for j in range(SJ):
                    pool.indirect_dma_start(
                        out, bass.IndirectOffsetOnAxis(ap=meta[b][:, j, 0:1].bitcast(i32), axis=0),
                        yw[:, j, :], None, compute_op=ALU.add).then_inc(added, 16)
            experts(pool, part)
            pool.wait_ge(added, 16 * SJ * E)

        @block.scalar
        def _(act):
            act.wait_ge(in_small, 16 * 5)

            def vcol(n):
                return vec[:, n:n + 1]

            def normed(g, par):
                wait(act, a_set, g + 1)
                wait(act, r2_set, g + 1)
                for j in range(J):
                    last = act.activation(an[:, j, :], a[par][:, j, :], ACT.Copy, scale=r2[:, j:j + 1])
                last.then_inc(an_set, 1)

            def xT(g):
                for k in range(KD):
                    wait(act, xT_full, KD * g + k + 1)
                    act.activation(xnT[:, k, :], bank[6 + k][:, :], ACT.Identity,
                                   scale=vcol(V_N1W + k), bias=vcol(V_N1B + k)).then_inc(xT_taken, 1)

            normed(0, 0)
            xT(0)

            def step(s, par, first, second, ahead, seq):
                p = s - 1

                def u(j):
                    if not second:
                        return
                    wait(act, u_full, NH * p + j + 1)
                    wait(act, prod_set, NH * p + max(j - 1, 0))
                    w = HW[j]
                    act.activation(su[0:w, j % 2, :], bank[4][0:w, :], ACT.Silu,
                                   bias=vec[0:w, V_BU + j:V_BU + j + 1]).then_inc(u_taken, 1)

                def take_ret(c):
                    if not first:
                        return
                    wait(act, ret_full, J * s + c + 1)
                    if c == 0:
                        wait(act, gn_set, 2 * s)
                    act.activation(ret[:, c, :], bank[6][:, 0:D], ACT.Copy).then_inc(ret_taken, 1)

                def squares(n):
                    if not first:
                        return
                    wait(act, xc_set, 2 * s + n + 1)
                    wait(act, gvar_set, 2 * s + n)
                    act.activation(sq[:, :, :], ret[:, 2 * n:2 * n + 2, :], ACT.Square).then_inc(sq_set, 1)

                if second:
                    for k in range(KD):
                        wait(act, x2T_full, KD * p + k + 1)
                        act.activation(x2T[:, k, :], bank[6 + k][:, :], ACT.Identity,
                                       scale=vcol(V_N2W + k), bias=vcol(V_N2B + k)).then_inc(x2T_taken, 1)
                if first:
                    wait(act, qk_taken, 4 * s + 4)
                    for o in range(4):
                        act.activation(kX[:, o, :, :], kT[:, :, :], ACT.Copy,
                                       scale=const[:, K_PAR + o:K_PAR + o + 1]).then_inc(kX_set, 1)
                    wait(act, gg_set, 2 * s)
                    for m in range(KD):
                        wait(act, gate_full, KD * s + m + 1)
                        act.activation(gateT[:, m, :], bank[4 + m][:, :], ACT.Silu, bias=vcol(V_BG + m)).then_inc(gate_taken, 1)
                    for i in range(2):
                        wait(act, kt_full, 2 * s + i + 1)
                        act.activation(ktok[:, 2 * i:2 * i + 2, :],
                                       bank[2 + i][:, :].rearrange("p (j d) -> p j d", j=2), ACT.Copy).then_inc(kt_taken, 1)
                u(0)
                u(1)
                take_ret(0)
                u(2)
                take_ret(1)
                u(3)
                squares(0)
                take_ret(2)
                take_ret(3)
                squares(1)
                u(4)
                u(5)
                if ahead:
                    normed(s + 1, 1 - par)
                if first:
                    for m in range(KD):
                        wait(act, gnT_full, KD * s + m + 1)
                        act.activation(gnT[:, m, :], bank[m][:, :], ACT.Identity,
                                       scale=vcol(V_GNW + m), bias=vcol(V_GNB + m)).then_inc(gnT_taken, 1)
                if ahead:
                    xT(s + 1)
                if second:
                    for k in range(KD):
                        wait(act, xtT_full, KD * p + k + 1)
                        act.activation(xtT[:, k, :], bank[4 + k][:, :], ACT.Copy).then_inc(xtT_taken, 1)
            steps(act, step)

            act.wait_ge(in_moe, 32)

            def part(e, b, first, last, n):
                def xe_high(e):
                    for k in range(KD):
                        wait(act, xeT_full, KD * e + k + 1)
                        act.activation(xeh[:, k, :], bank[4 + k][:, 0:CP], ACT.Copy).then_inc(xeh_set, 1)

                def w1_high(e):
                    wait(act, w1_in, 16 * (e + 1))
                    wait(act, h1_full, MF * e)
                    for k in range(KD):
                        act.activation(W1h[:, k, :], W1[:, k, :], ACT.Copy).then_inc(w1h_set, 1)

                def w2_high(e, k):
                    if k == 0:
                        wait(act, w2_in, 16 * (e + 1))
                        wait(act, y_full, KD * e)
                    act.activation(W2h[:, 4 * k:4 * k + 4, :], W2[:, 4 * k:4 * k + 4, :], ACT.Copy).then_inc(w2h_set, 1)

                def weighted(e, b):
                    wait(act, added, 16 * SJ * e)
                    wait(act, meta_set, e + 1)
                    for j in range(SJ):
                        wait(act, yt_full, SJ * e + max(j + 1, 2))
                        act.activation(yw[:, j, :], bank[4 + j // 2][0:SP_, (j % 2) * D:(j % 2 + 1) * D], ACT.Copy,
                                       scale=meta[b][:, j, 1:2]).then_inc(yt_taken, 1)

                if first:
                    w1_high(0)
                    xe_high(0)
                for m in range(MF):
                    wait(act, h1_full, MF * e + m + 1)
                    wait(act, hel_set, MF * e + m - 1 if m > 1 or not first else 0)
                    act.activation(he[:, m % 2, :], bank[m % 4][:, 0:CP], ACT.Gelu,
                                   bias=B1_col(e, m)).then_inc(h1_taken, 1)
                    if m == 0 or m == 2:
                        w2_high(e, m // 2)
                    if m == 4 and not first:
                        weighted(e - 1, 1 - b)
                if not last:
                    w1_high(e + 1)
                    xe_high(e + 1)
                else:
                    weighted(e, b)

            def B1_col(e, m):
                return B1[:, :, :].rearrange("p e m -> p (e m)")[:, bass.ds(e * MF + m, 1)]
            experts(act, part)

        @block.vector
        def _(dve):
            dve.memset(vz[:, :, :], 0.0).then_inc(strict_set, 1)
            dve.wait_ge(in_small, 16 * 5)
            dve.tensor_copy(strict[:, :], const[:, K_STRICT:K_IOTA]).then_inc(strict_set, 1)
            dve.tensor_copy(tokf[:, :], tok0).then_inc(strict_set, 1)
            dve.wait_ge(consts_set, 4)

            def stats(x, st, mv, done, n_bn):
                for j in range(J):
                    last = dve.bn_stats(st[:, j, :], x[:, j, :])
                last.then_inc(bn, 1)
                wait_apart(dve, bn, n_bn)
                for j in range(J):
                    last = dve.bn_aggr(mv[:, j, :], st[:, j, :])
                last.then_inc(done, 1)

            def bn_count(s, ahead, which):
                n = 1 + 2 * s
                return n + ahead + which

            def head_stats(g, par, n_bn):
                wait(dve, h_set, g + 1)
                stats(hres[par], st_h, mv_h, stats_h, n_bn)

            def head_norm(g, par):
                wait(dve, r1_set, g + 1)
                wait(dve, hx_add, g - 1)
                for j in range(J):
                    last = dve.tensor_scalar(a[par][:, j, :], hres[par][:, j, :], mv_h[:, j, 0:1], r1[:, j:j + 1],
                                             ALU.subtract, ALU.mult)
                last.then_inc(a_set, 1)

            head_stats(0, 0, 1)
            head_norm(0, 0)

            def place_rows(s):
                if isinstance(s, int) and s < 2:
                    return
                q = s - 2
                wait(dve, cnt_full, q + 1)
                dve.tensor_tensor(ohc[:, :, :].rearrange("p (j k) e -> p j k e", k=2),
                                  bank[5][:, 0:J * E].rearrange("p (j e) -> p j e", j=J).unsqueeze(2).to_broadcast([P, J, 2, E]),
                                  oh[:, :, :].rearrange("p (j k) e -> p j k e", k=2), ALU.mult).then_inc(cnt_taken, 1)
                dve.tensor_reduce(osg[:, :], osum[:, :, :].rearrange("p j e -> p e j"), AX.X, ALU.add).then_inc(route, 1)
                dve.wait_ge(cnt_taken, q + 1)
                dve.tensor_reduce(pos, ohc[:, :, :], AX.X, ALU.add).then_inc(route, 1)
                dve.wait_ge(route, 7 * q + 5)
                dve.tensor_tensor(oacc[:, :], oacc[:, :], osg[:, :], ALU.add).then_inc(oacc_set, 1)
                dve.scalar_tensor_tensor(slf, idf[:, :, :].rearrange("p j k -> p (j k)"), float(CP), pos,
                                         ALU.mult, ALU.add).then_inc(route, 1)
                dve.tensor_scalar(over, pos, float(C), 1e6, ALU.is_ge, ALU.mult).then_inc(route, 1)
                dve.wait_ge(route, 7 * q + 7)
                dve.tensor_tensor(slot[:, :], slf, over, ALU.add).then_inc(slot_set, 1)

            def step(s, par, first, second, ahead, seq):
                p = s - 1

                def glu(j):
                    if not second:
                        return
                    w = HW[j]
                    wait(dve, g_full, NH * p + j + 1)
                    wait(dve, u_taken, NH * p + j + 1)
                    dve.scalar_tensor_tensor(prodT[0:w, j, :], bank[5][0:w, :], vec[0:w, V_BGL + j:V_BGL + j + 1],
                                             su[0:w, j % 2, :], ALU.add, ALU.mult).then_inc(prod_set, 1)

                def mask(c):
                    if not first:
                        return
                    for q in range(4):
                        wait(dve, sc_full, 16 * s + 4 * c + q + 1)
                        dve.tensor_tensor(sm[:, q, :, :], bank[q][:, :].rearrange("p (h n) -> p h n", h=4),
                                          causal.unsqueeze(1).to_broadcast([P, 4, P]), ALU.mult).then_inc(sc_masked, 1)

                def next_state(c):
                    if not first:
                        return
                    wait(dve, kv_full, J * s + c + 1)
                    if par == 0 and c == 0:
                        dve.tensor_tensor(state[:, :], bank[7][:, 0:D], bd_tab, ALU.mult).then_inc(state_set, 1)
                        return
                    dve.tensor_tensor(stmp[:, :], bank[7][:, 0:D], state[:, :], ALU.add).then_inc(kv_added, 1)
                    dve.wait_ge(kv_added, seq * 7 + (4 * par + c))
                    dve.tensor_tensor(state[:, :], stmp[:, :], bd_tab, ALU.mult).then_inc(state_set, 1)

                def gn_mean(n):
                    if not first:
                        return
                    r4 = ret[:, 2 * n:2 * n + 2, :].rearrange("p j (h d) -> p (j h) d", h=H)
                    gs = gsum[:, 32 * n:32 * n + 32]
                    wait(dve, ret_taken, J * s + 2 * n + 2)
                    dve.tensor_reduce(gs, r4, AX.X, ALU.add).then_inc(gsum_set, 1)
                    wait(dve, gsum_set, 2 * s + n + 1)
                    dve.scalar_tensor_tensor(r4, gs.unsqueeze(2).to_broadcast([P, 32, HD]), -1.0 / HD, r4,
                                             ALU.mult, ALU.add).then_inc(xc_set, 1)

                def gn_var(n):
                    if not first:
                        return
                    wait(dve, sq_set, 2 * s + n + 1)
                    if n == 0:
                        wait(dve, grst_set, 2 * s)
                    dve.tensor_reduce(gvar[:, 32 * n:32 * n + 32],
                                      sq[:, :, :].rearrange("p j (h d) -> p (j h) d", h=H), AX.X, ALU.add).then_inc(gvar_set, 1)

                if not first:
                    place_rows(s)
                if first:
                    for n in range(4):
                        w, m = n // 2, n % 2
                        if n == 2:
                            place_rows(s)
                        wait(dve, qk_full, 4 * s + n + 1)
                        dve.scalar_tensor_tensor(
                            (qT, kT)[w][:, m, :].rearrange("p (j n) -> p j n", j=J),
                            bank[n][:, :].rearrange("p (j n) -> p j n", j=J),
                            vec[:, (V_BQ, V_BK)[w] + m:(V_BQ, V_BK)[w] + m + 1],
                            (q_tab, k_tab)[w][:, m, :].unsqueeze(1).to_broadcast([P, J, P]),
                            ALU.add, ALU.mult).then_inc(qk_taken, 1)
                    for i in range(2):
                        wait(dve, v_full, 2 * s + i + 1)
                        for jj in range(2):
                            last = dve.tensor_tensor(own_columns(2 * i + jj, 0, 4),
                                                     bank[i][:, jj * D:(jj + 1) * D].rearrange("p (g r d) -> p g r d", g=4, r=4),
                                                     row[:, 0, :].rearrange("p (g r d) -> p g r d", g=4, r=4), ALU.add)
                        last.then_inc(v_taken, 1)
                glu(0)
                mask(0)
                glu(1)
                if ahead:
                    head_stats(s + 1, 1 - par, bn_count(s, ahead, 0))
                next_state(0)
                mask(1)
                glu(2)
                next_state(1)
                mask(2)
                glu(3)
                gn_mean(0)
                next_state(2)
                mask(3)
                gn_var(0)
                next_state(3)
                gn_mean(1)
                gn_var(1)
                glu(4)
                if ahead:
                    head_norm(s + 1, 1 - par)
                glu(5)
                if first:
                    for n in range(2):
                        wait(dve, grst_set, 2 * s + n + 1)
                        dve.tensor_tensor(gn[:, 2 * n:2 * n + 2, :].rearrange("p j (h d) -> p (j h) d", h=H),
                                          ret[:, 2 * n:2 * n + 2, :].rearrange("p j (h d) -> p (j h) d", h=H),
                                          grst[:, 32 * n:32 * n + 32].unsqueeze(2).to_broadcast([P, 32, HD]),
                                          ALU.mult).then_inc(gn_set, 1)
                def gated():
                    if not first:
                        return
                    for m in range(KD):
                        wait(dve, gnT_taken, KD * s + m + 1)
                        dve.tensor_tensor(gnT[:, m, :], gnT[:, m, :], gateT[:, m, :], ALU.mult).then_inc(gg_set, 1)

                def next_rows(i):
                    wait(dve, r_3_set, 2 * p + i + 1)
                    if i == 0:
                        dve.wait_ge(slots_empty, 32)
                        wait(dve, scattered, 16 * 2 * J * p)
                    for j in (2 * i, 2 * i + 1):
                        last = dve.tensor_scalar(pl[:, j, :, 0:D], hf[:, j, :].unsqueeze(1).to_broadcast([P, 2, D]),
                                                 mv_3[:, j, 0:1], r_3[:, j:j + 1], ALU.subtract, ALU.mult)
                    last.then_inc(xt_set, 1)

                if not second:
                    gated()
                if second:
                    wait(dve, hx_set, s)
                    for i in range(2):
                        wait(dve, o_full, 2 * p + i + 1)
                        dve.tensor_tensor(hf[:, 2 * i:2 * i + 2, :], bank[4 + i][:, :].rearrange("p (j d) -> p j d", j=2),
                                          hf[:, 2 * i:2 * i + 2, :], ALU.add).then_inc(hf_set, 1)
                        dve.wait_ge(hf_set, 2 * p + i + 1)
                        for j in (2 * i, 2 * i + 1):
                            last = dve.bn_stats(st_3[:, j, :], hf[:, j, :])
                        last.then_inc(bn_3, 1)
                        wait_apart(dve, bn_3, 2 * p + i + 1)
                        for j in (2 * i, 2 * i + 1):
                            last = dve.bn_aggr(mv_3[:, j, :], st_3[:, j, :])
                        last.then_inc(stats_3, 1)
                        if i == 0:
                            gated()
                        next_rows(i)
                def residual(i):
                    if not first:
                        return
                    if i == 0:
                        wait(dve, abo_set, s + 1)
                    wait(dve, wo_full, 2 * s + i + 1)
                    dve.tensor_tensor(a[par][:, 2 * i:2 * i + 2, :], bank[2 + i][:, :].rearrange("p (j d) -> p j d", j=2),
                                      a[par][:, 2 * i:2 * i + 2, :], ALU.add).then_inc(wo_taken, 1)
                residual(0)
                residual(1)
                if first:
                    wait(dve, wo_taken, 2 * s + 2)
                    stats(a[par], st_2, mv_2, stats_2, bn_count(s, ahead, 1))
                if second:
                    wait(dve, lg_full, s)
                    dve.tensor_tensor(lgs[:, :, :], bank[4][:, 0:J * E].rearrange("p (j e) -> p j e", j=J),
                                      gb[:, :].unsqueeze(1).to_broadcast([P, J, E]), ALU.add).then_inc(lg_taken, 1)
                    wait_apart(dve, lg_taken, s)
                    for j in range(J):
                        last = dve.max(m8[:, j, :], lgs[:, j, :])
                    last.then_inc(top_set, 1)
                    wait(dve, top_set, 2 * p + 1)
                    dve.tensor_tensor(dl, m8[:, :, 1], m8[:, :, 0], ALU.subtract).then_inc(dl_set, 1)
                    for j in range(J):
                        last = dve.max_index(i8[:, j, :], m8[:, j, :], lgs[:, j, :])
                    last.then_inc(top_set, 1)
                    wait(dve, top_set, 2 * p + 2)
                    dve.tensor_copy(idf[:, :, :], i8[:, :, 0:2]).then_inc(route, 1)
                    dve.wait_ge(route, 7 * p + 1)
                    dve.tensor_tensor(oh[:, :, :], iota.unsqueeze(1).to_broadcast([P, J * 2, E]),
                                      idf[:, :, :].rearrange("p j k -> p (j k)").unsqueeze(2).to_broadcast([P, J * 2, E]),
                                      ALU.is_equal).then_inc(oh_set, 1)
                    wait(dve, oh_set, s)
                    o4 = oh[:, :, :].rearrange("p (j k) e -> p j k e", k=2)
                    dve.tensor_tensor(osum[:, :, :], o4[:, :, 0, :], o4[:, :, 1, :], ALU.add).then_inc(osum_set, 1)
                if second:
                    wait(dve, ed_set, s)
                    dve.tensor_scalar(den, ed, 1.0, None, ALU.add).then_inc(route, 1)
                    dve.wait_ge(route, 7 * p + 2)
                    dve.reciprocal(wt1, den).then_inc(route, 1)
                    dve.wait_ge(route, 7 * p + 3)
                    dve.tensor_copy(pl[:, :, 0, D + 1], wt1)
                    dve.tensor_tensor(pl[:, :, 1, D + 1], ed, wt1, ALU.mult)
                    dve.tensor_copy(pl[:, :, :, D].bitcast(i32), tokf[:, :].rearrange("p (j k) -> p j k", k=2)).then_inc(wt_set, 1)
                    wait(dve, wt_set, s)
                    dve.tensor_scalar(tokf[:, :], tokf[:, :], float(GT), None, ALU.add)
                if first:
                    wait(dve, r_2_set, s + 1)
                    for j in range(J):
                        last = dve.tensor_scalar(x2n[:, j, :], a[par][:, j, :], mv_2[:, j, 0:1], r_2[:, j:j + 1],
                                                 ALU.subtract, ALU.mult)
                    last.then_inc(x2n_set, 1)

            steps(dve, step)
            place_rows(G + 1)

            def part(e, b, first, last, n):
                def xe_low(e):
                    for k in range(KD):
                        wait(dve, xeh_set, KD * e + k + 1)
                        dve.tensor_tensor(xel[:, k, :], bank[4 + k][:, 0:CP], xeh[:, k, :].bitcast(f32),
                                          ALU.subtract).then_inc(xel_set, 1)

                def w1_low(e):
                    for k in range(KD):
                        wait(dve, w1h_set, KD * e + k + 1)
                        dve.tensor_tensor(W1l[:, k, :], W1[:, k, :], W1h[:, k, :].bitcast(f32),
                                          ALU.subtract).then_inc(w1l_set, 1)

                def w2_low(e):
                    wait(dve, w2h_set, KD * e + 1)
                    t = slice(0, MF // 2)
                    dve.tensor_tensor(W2l[:, t, :], W2[:, t, :], W2h[:, t, :].bitcast(f32), ALU.subtract).then_inc(w2l_set, 1)

                if first:
                    w1_low(0)
                    xe_low(0)
                for m in range(MF):
                    wait(dve, h1_taken, MF * e + m + 1)
                    dve.tensor_copy(heh[:, m, :], he[:, m % 2, :]).then_inc(heh_set, 1)
                    wait(dve, heh_set, MF * e + m + 1)
                    dve.tensor_tensor(hel[:, m, :], he[:, m % 2, :], heh[:, m, :].bitcast(f32), ALU.subtract).then_inc(hel_set, 1)
                    if m == 2:
                        w2_low(e)
                if not last:
                    w1_low(e + 1)
                for k in range(KD):
                    if k == 1 and not last:
                        xe_low(e + 1)
                    wait(dve, y_full, KD * e + k + 1)
                    if k == 0:
                        wait(dve, yt_full, SJ * e)
                    dve.tensor_scalar(yT[:, k, :], bank[6 + k][:, 0:CP],
                                      B2[:, :, :].rearrange("p e k -> p (e k)")[:, bass.ds(e * KD + k, 1)], None,
                                      ALU.add).then_inc(y_taken, 1)
            dve.wait_ge(in_moe, 32)
            experts(dve, part)

        @block.tensor
        def _(pe):
            pe.wait_ge(in_small, 16 * 5)
            pe.wait_ge(strict_set, 3)
            pe.wait_ge(consts_set, 4)

            def mm(o, l, r, start, stop, loose=False):
                return pe.matmul(o, l, r, start=start, stop=stop, skip_group_check=loose)

            def xT(g):
                wait(pe, an_set, g + 1)
                wait(pe, ret_taken, J * g)
                wait(pe, state_set, J * g)
                for k in range(KD):
                    for j in range(J):
                        last = pe.transpose(bank[6 + k][:, j * P:(j + 1) * P], an[:, j, k * P:(k + 1) * P], ident)
                    last.then_inc(xT_full, 1)

            xT(0)
            pe.wait_ge(in_w, 16 * 5)

            def count(s):
                if isinstance(s, int) and s < 2:
                    return
                wait(pe, osum_set, s - 1)
                wait(pe, oacc_set, s - 2)
                wait(pe, xtT_taken, KD * (s - 1))
                for j in range(J):
                    o = bank[5][:, j * E:(j + 1) * E]
                    mm(o, strict[:, :], osum[:, j, :], True, False)
                    for i in range(j):
                        mm(o, ones[:, :], osum[:, i, :], False, False)
                    last = mm(o, ones[:, :], oacc[:, :], False, True)
                last.then_inc(cnt_full, 1)

            def step(s, par, first, second, ahead, seq):
                p = s - 1

                def glu(j):
                    if not second:
                        return
                    w = HW[j]
                    if j == 0:
                        wait(pe, x2T_taken, KD * s)
                        if first:
                            wait(pe, gate_taken, KD * (s + 1))
                        else:
                            wait(pe, lg_taken, p)
                            wait(pe, cnt_taken, p)
                    wait(pe, u_taken, NH * p + j)
                    for k in range(KD):
                        last = mm(bank[4][0:w, :], Win[:, k, j * P:j * P + w], x2T[:, k, :], k == 0, k == KD - 1)
                    last.then_inc(u_full, 1)
                    wait(pe, prod_set, NH * p + j)
                    for k in range(KD):
                        last = mm(bank[5][0:w, :], Win[:, k, HID + j * P:HID + j * P + w], x2T[:, k, :], k == 0, k == KD - 1)
                    last.then_inc(g_full, 1)

                def score(c, q):
                    if c == 0:
                        if q < 2:
                            wait(pe, v_taken, 2 * s + q + 1)
                        else:
                            wait(pe, kt_taken, 2 * s + q - 1)
                    else:
                        wait(pe, sc_masked, 16 * s + 4 * (c - 1) + q + 1)
                    rows_ = slice(64 * (q % 2), 64 * (q % 2) + 64)
                    t = slice(c * P, (c + 1) * P)
                    for n in range(4):
                        last = mm(bank[q][:, n * P:(n + 1) * P], kX[rows_, n, q // 2, t], qT[rows_, q // 2, t], True, True)
                    last.then_inc(sc_full, 1)

                def chunk(c):
                    t = slice(c * P, (c + 1) * P)
                    empty_state = par == 0 and c == 0
                    if c > 0:
                        wait(pe, ret_taken, J * s + c)
                    if not empty_state:
                        wait(pe, state_set, J * s + c)
                        for m in range(KD):
                            mm(bank[6][:, m * P:(m + 1) * P], qT[:, m, t], state[:, m * P:(m + 1) * P], m == 0, False, True)
                    for m in range(KD):
                        last = mm(bank[7][:, m * P:(m + 1) * P], ktok[:, c, m * P:(m + 1) * P], own_columns(c, 2 * m, 2),
                                  True, True)
                    last.then_inc(kv_full, 1)
                    for q in range(4):
                        wait(pe, sc_masked, 16 * s + 4 * c + q + 1)
                        for n in range(4):
                            h = 4 * q + n
                            last = mm(bank[6][:, h // 4 * 64:h // 4 * 64 + 64], sm[:, q, n, :], vz[:, c, h * 64:h * 64 + 64],
                                      empty_state and q == 0 and n == 0, q == 3 and n == 3, True)
                        if q == 3:
                            last.then_inc(ret_full, 1)
                        if c < J - 1:
                            score(c + 1, q)

                if first:
                    wait(pe, xT_taken, KD * (s + 1))
                    for n in range(4):
                        W, m = (Wq, Wk)[n // 2], n % 2
                        if n == 0:
                            wait(pe, gnT_taken, KD * s)
                        if n == 2:
                            count(s)
                            wait(pe, wo_taken, 2 * s)
                        for k in range(KD):
                            last = mm(bank[n][:, :], W[:, k, m * P:(m + 1) * P], xnT[:, k, :], k == 0, k == KD - 1)
                        last.then_inc(qk_full, 1)
                else:
                    count(s)
                if second:
                    wait(pe, x2n_set, s)
                    for k in range(KD):
                        for j in range(J):
                            last = pe.transpose(bank[6 + k][:, j * P:(j + 1) * P], x2n[:, j, k * P:(k + 1) * P], ident)
                        last.then_inc(x2T_full, 1)
                if first:
                    wait(pe, lg_taken, p)
                    wait(pe, cnt_taken, p)
                    for m in range(KD):
                        for k in range(KD):
                            last = mm(bank[4 + m][:, :], Wg[:, k, m * P:(m + 1) * P], xnT[:, k, :], k == 0, k == KD - 1)
                        last.then_inc(gate_full, 1)
                    for i in range(2):
                        wait(pe, qk_taken, 4 * s + i + 1)
                        for jj in range(2):
                            j = 2 * i + jj
                            for k in range(KD):
                                last = mm(bank[i][:, jj * D:(jj + 1) * D], xnT[:, k, j * P:(j + 1) * P], Wv[:, k, :],
                                          k == 0, k == KD - 1)
                        last.then_inc(v_full, 1)
                    wait(pe, qk_taken, 4 * s + 4)
                    for i in range(2):
                        for jj in range(2):
                            j = 2 * i + jj
                            for m in range(KD):
                                last = pe.transpose(bank[2 + i][:, jj * D + m * P:jj * D + (m + 1) * P],
                                                    kT[:, m, j * P:(j + 1) * P], ident)
                        last.then_inc(kt_full, 1)
                if second and isinstance(s, int) and s == 1 or not isinstance(s, int):
                    pe.wait_ge(in_ffn, 48)
                glu(0)
                if first:
                    wait(pe, kX_set, 4 * (s + 1))
                    for q in range(4):
                        score(0, q)
                    if second:
                        wait(pe, x2T_taken, KD * s)
                    wait(pe, kt_taken, 2 * (s + 1))
                    wait(pe, v_taken, 2 * (s + 1))
                for c in range(J):
                    if c < J - 1:
                        glu(c + 1)
                    if first:
                        chunk(c)
                glu(NH - 2)
                glu(NH - 1)
                def ffn_out(i):
                    if not second:
                        return
                    if i == 0:
                        wait(pe, u_taken, NH * s)
                    for jj in range(2):
                        j = 2 * i + jj
                        for n in range(NH):
                            w = HW[n]
                            if j == 0:
                                wait(pe, prod_set, NH * p + max(n + 1, NH - 1))
                            last = mm(bank[4 + i][:, jj * D:(jj + 1) * D], prodT[0:w, n, j * P:(j + 1) * P],
                                      Wout[0:w, n, :], n == 0, n == NH - 1)
                    last.then_inc(o_full, 1)
                ffn_out(0)
                if first:
                    wait(pe, gn_set, 2 * (s + 1))
                    wait(pe, sc_masked, 16 * (s + 1))
                    for m in range(KD):
                        for j in range(J):
                            last = pe.transpose(bank[m][:, j * P:(j + 1) * P], gn[:, j, m * P:(m + 1) * P], ident)
                        last.then_inc(gnT_full, 1)
                ffn_out(1)

                def out_proj(j):
                    if not first:
                        return
                    wait(pe, gg_set, KD * (s + 1))
                    for m in range(KD):
                        last = mm(bank[2 + j // 2][:, j % 2 * D:(j % 2 + 1) * D], gnT[:, m, j * P:(j + 1) * P], Wo[:, m, :],
                                  m == 0, m == KD - 1)
                    if j % 2:
                        last.then_inc(wo_full, 1)

                if ahead:
                    xT(s + 1)
                out_proj(0)
                out_proj(1)
                out_proj(2)
                if second:
                    wait(pe, xt_set, 2 * s)
                    wait(pe, hf_set, 2 * s)
                    for k in range(KD):
                        for j in range(J):
                            last = pe.transpose(bank[4 + k][:, j * P:(j + 1) * P], pl[:, j, 0, k * P:(k + 1) * P], ident)
                        last.then_inc(xtT_full, 1)
                out_proj(3)
                if second:
                    wait(pe, xtT_taken, KD * s)
                    for j in range(J):
                        for k in range(KD):
                            last = mm(bank[4][:, j * E:(j + 1) * E], xtT[:, k, j * P:(j + 1) * P], Gw[:, k, :], k == 0, k == KD - 1)
                    last.then_inc(lg_full, 1)
            steps(pe, step)
            count(G + 1)

            def part(e, b, first, last, n):
                def to_features(e, b, n):
                    wait(pe, xr_in[b], 16 * n)
                    wait(pe, yt_taken, SJ * (e - 1) if not first or e else 0)
                    for k in range(KD):
                        for j in range(SJ):
                            ins = pe.transpose(bank[4 + k][:, j * SP_:(j + 1) * SP_], xr[b][:, j, k * P:(k + 1) * P],
                                               const[0:SP_, K_ID:K_ID + SP_])
                        ins.then_inc(xeT_full, 1)

                def to_tokens(e):
                    wait(pe, y_taken, KD * (e + 1))
                    wait(pe, xel_set, KD * (e + 2) if not last or not same(e) else KD * E)
                    for j in range(SJ):
                        for k in range(KD):
                            ins = pe.transpose(bank[4 + j // 2][0:SP_, (j % 2) * D + k * P:(j % 2) * D + (k + 1) * P],
                                               yT[:, k, j * SP_:(j + 1) * SP_], ident)
                        ins.then_inc(yt_full, 1)

                def same(x):
                    return isinstance(x, int) and x == E - 1

                def product(o, high, low, n, steps):
                    for k in range(steps):
                        n(k)
                        (ah, bh), (al, bl) = high(k), low(k)
                        for t, (x, y) in enumerate(((ah, bh), (ah, bl), (al, bh))):
                            ins = mm(o, x, y, k == 0 and t == 0, k == steps - 1 and t == 2)
                    return ins

                if first:
                    to_features(0, 0, 1)
                wait(pe, w1l_set, KD * (e + 1))
                wait(pe, xel_set, KD * (e + 1))
                for m in range(MF):
                    wait(pe, h1_taken, MF * e + m - 3 if m > 3 or not first else 0)
                    t = slice(m * P, (m + 1) * P)
                    product(bank[m % 4][:, 0:CP], lambda k: (W1h[:, k, t], xeh[:, k, :]),
                            lambda k: (W1l[:, k, t], xel[:, k, :]), lambda k: None, KD).then_inc(h1_full, 1)
                    if m == 3 and not first:
                        to_tokens(e - 1)

                def second_operands(m):
                    wait(pe, (w2l_set, w2l_also)[m // (MF // 2)], e + 1)
                    wait(pe, hel_set, MF * e + m + 1)

                for k in range(KD):
                    if k == 1 and not last:
                        to_features(e + 1, 1 - b, n if b == 0 else n + 1)
                    t = slice(k * P, (k + 1) * P)
                    wait(pe, y_taken, KD * e)
                    product(bank[6 + k][:, 0:CP], lambda m: (W2h[:, m, t], heh[:, m, :]),
                            lambda m: (W2l[:, m, t], hel[:, m, :]),
                            second_operands if k == 0 else lambda m: None, MF).then_inc(y_full, 1)
                if last:
                    to_tokens(e)

            experts(pe, part)


def kernel(**x):
    import concourse.bacc as _bacc
    from concourse.bass_utils import run_bass_kernel_spmd as _run

    def get(name):
        return np.asarray(x[name])

    def columns(a, n):
        a = np.concatenate([a, np.zeros(n * P - a.shape[0], a.dtype)])
        return a.reshape(n, P).T

    A, M = "L0_attn_", "L0_ffn_"
    consts, empty = shape_constants()
    b_in = get(A + "b_in")
    vecs = np.concatenate(
        [columns(get(A + n), KD) for n in ("norm1_w", "norm1_b", "bq", "bk", "bg", "gn_w", "gn_b", "norm2_w", "norm2_b")]
        + [columns(b_in[:HID], NH), columns(b_in[HID:], NH)], axis=1)
    arrays = {
        "idx": get("x").reshape(G, J, P).transpose(0, 2, 1),
        "emb": get("L0_tok_emb_table"),
        "consts": consts, "empty": empty, "vecs": vecs,
        "rows": np.stack([get(A + n) for n in ("bv", "bo", "b_out")]),
        **{n: get(A + n) for n in ("wq", "wk", "wv", "wg", "wo", "w_in", "w_out")},
        "gate_w": get(M + "gate_w"), "gate_b": get(M + "gate_b"),
        "w1": get(M + "w1").reshape(E, KD, P, F).transpose(0, 2, 1, 3),
        "b1": get(M + "b1").reshape(E, MF, P).transpose(2, 0, 1),
        "w2": get(M + "w2").reshape(E, MF, P, D).transpose(0, 2, 1, 3),
        "b2": get(M + "b2").reshape(E, KD, P).transpose(2, 0, 1),
    }
    arrays = {n: np.ascontiguousarray(v) for n, v in arrays.items()}
    nc = _bacc.Bacc("TRN2", target_bir_lowering=False, num_devices=1)
    args = [nc.dram_tensor(n, v.shape, mybir.dt.from_np(v.dtype), kind="ExternalInput").ap() for n, v in arrays.items()]
    out = nc.dram_tensor("out", [T + DUMP, D], f32, kind="ExternalOutput").ap()
    xe = nc.dram_tensor("xe", [E * CP, ROW], f32, kind="Internal").ap()
    build(nc, *args, out, xe)
    r = _run(nc, [arrays], core_ids=[0])
    return r.results[0]["out"][:T].reshape(B, S, D)
```

```python
import concourse.bass as bass
from concourse import mybir
from contextlib import ExitStack
import numpy as np

f32 = mybir.dt.float32
f32r = mybir.dt.float32r
bf16 = mybir.dt.bfloat16
i32 = mybir.dt.int32
u32 = mybir.dt.uint32
ALU = mybir.AluOpType
ACT = mybir.ActivationFunctionType
AX = mybir.AxisListType

P = 128
B, S, D = 4, 1024, 256
T = B * S
KD = D // P
H, HD = 16, 16
J = 4
GT = J * P
G = T // GT
HID = 682
NH = -(-HID // P)
HW = [min(P, HID - n * P) for n in range(NH)]
E, F, C = 32, 1024, 308
MF = F // P
SP_ = 104
SJ = 3
CP = SP_ * SJ
SR = [min(SP_, C - j * SP_) for j in range(SJ)]
ROW = D + 2
EPS = 1e-5
HEADS_NORMED = ((0, 2), (2, 3), (3, 4))
NN = len(HEADS_NORMED)
DUMP = CP

V_N1W, V_N1B, V_BQ, V_BK, V_BG, V_GNW, V_GNB, V_N2W, V_N2B = range(0, 18, 2)
V_BU = 18
V_BGL = V_BU + NH
V_ALL = V_BGL + NH

K_Q = 0
K_K = K_Q + KD * P
K_BD = K_K + KD * P
K_CAUSAL = K_BD + KD * P
K_ID = K_CAUSAL + P
K_STRICT = K_ID + P
K_IOTA = K_STRICT + P
K_TOK = K_IOTA + E
K_PAR = K_TOK + 8
K_ALL = K_PAR + 4


def shape_constants():
    c = np.zeros((P, K_ALL), np.float32)
    p = np.arange(P)
    pos = np.arange(S, dtype=np.float32)
    inv = np.power(np.float32(10000.0), (np.float32(-2.0) * np.arange(D // 2, dtype=np.float32) / np.float32(D))).astype(np.float32)
    ang = (pos[:, None] * inv[None, :]).astype(np.float32).astype(np.float64)
    pe = np.stack([np.sin(ang), np.cos(ang)], -1).reshape(S, D)
    gamma = 1.0 - 2.0 ** (-5.0 - np.arange(H))
    feature = np.arange(D).reshape(KD, P)
    gf = gamma[feature // HD].T
    c[:, K_Q:K_K] = (HD ** -0.5 * gf[:, :, None] ** p[None, None, :]).reshape(P, -1)
    c[:, K_K:K_BD] = (gf[:, :, None] ** -p[None, None, :].astype(np.float64)).reshape(P, -1)
    same = (p[:, None] // HD == p[None, :] // HD)
    c[:, K_BD:K_CAUSAL] = (gf[:, :, None] ** P * same[:, None, :]).reshape(P, -1)
    c[:, K_CAUSAL:K_ID] = p[:, None] <= p[None, :]
    c[:, K_ID:K_STRICT] = np.eye(P)
    c[:, K_STRICT:K_IOTA] = p[:, None] < p[None, :]
    c[:, K_IOTA:K_TOK] = np.arange(E)[None, :]
    c[:, K_TOK:K_PAR] = (np.arange(J)[None, :, None] * P + p[:, None, None] + np.zeros((1, 1, 2))).reshape(P, -1)
    c[:, K_PAR:K_ALL] = (p[:, None] // HD) % 4 == np.arange(4)
    empty = np.zeros((SP_, SJ, ROW), np.float32)
    empty[:, :, D] = (T + np.arange(CP, dtype=np.int32).reshape(SP_, SJ)).astype(np.int32).view(np.float32)
    return c, pe.reshape(S // GT, J, P, D).transpose(0, 2, 1, 3), empty


def build(nc, idx, emb, consts, positions, empty, vecs, rows, wq, wk, wv, wg, wo, w_in, w_out, gate_w, gate_b, w1, b1, w2, b2,
          out, xe):
    ctx = ExitStack()
    with ctx:
        place = [ctx]

        def sb(name, shape, dt=f32):
            return place[-1].enter_context(nc.sbuf_tensor(name, shape, dt))

        def sem(name):
            return ctx.enter_context(nc.semaphore(name))

        const = sb("const", [P, K_ALL])
        vec = sb("vec", [P, V_ALL])
        row = sb("row", [P, 3, D])
        gb = sb("gb", [P, E])
        B1 = sb("B1", [P, E, MF])
        B2 = sb("B2", [P, E, KD])

        place.append(ExitStack())
        (Wqh, Wql), (Wkh, Wkl), (Wvh, Wvl), (Wgh, Wgl) = (
            [sb(n + part, [P, KD, D], f32r) for part in "hl"] for n in ("Wq", "Wk", "Wv", "Wg"))
        Wo = sb("Wo", [P, KD, D])
        kX = sb("kX", [P, 2, 4, KD, P])
        Winh, Winl = (sb(n, [P, KD, 2 * HID], f32r) for n in ("Winh", "Winl"))
        Wouth, Woutl = (sb(n, [P, NH, D], f32r) for n in ("Wouth", "Woutl"))
        Gw = sb("Gw", [P, KD, E])
        strict = sb("strict", [P, P], bf16)
        ones = sb("ones", [P, P], bf16)
        half = sb("half", [P, 64])
        euler = sb("euler", [P, J])

        q_tab = const[:, K_Q:K_K].rearrange("p (m n) -> p m n", m=KD)
        k_tab = const[:, K_K:K_BD].rearrange("p (m n) -> p m n", m=KD)
        bd_tab = const[:, K_BD:K_CAUSAL]
        causal = const[:, K_CAUSAL:K_ID]
        ident = const[:, K_ID:K_STRICT]
        iota = const[:, K_IOTA:K_TOK]
        tok0 = const[:, K_TOK:K_PAR]

        idxg = sb("idxg", [P, J], i32)
        hres = [sb(f"hres{n}", [P, J, D]) for n in range(2)]
        a = [sb(f"a{n}", [P, J, D]) for n in range(2)]
        an = sb("an", [P, J, D])
        pe_tab = sb("pe_tab", [P, J, D])
        xnT = sb("xnT", [P, KD, GT])
        xnh, xnl = (sb(n, [P, KD, GT], f32r) for n in ("xnh", "xnl"))
        qT = sb("qT", [P, KD, GT])
        kT = sb("kT", [P, KD, GT])
        gateT = sb("gateT", [P, KD, GT])
        vz = sb("vz", [P, J, H * 4 * HD])
        ktok = xnT[:, :, :].rearrange("p k n -> p (k n)").rearrange("p (j d) -> p j d", j=J)
        sm = sb("sm", [P, J, 4, P])
        state = sb("state", [P, KD * P])
        stmp = sb("stmp", [P, KD * P])
        ret = sb("ret", [P, J, D])
        sq = kT[:, 0, :].rearrange("p (j d) -> p j d", j=2)
        gn = ret
        gnT = kT
        x2n = an
        x2T = sb("x2T", [P, KD, GT])
        su = sb("su", [P, 2, GT])
        place.append(ExitStack())
        Wq, Wk, Wg, Wv = (sb(n, [P, KD, D]) for n in ("Wq", "Wk", "Wg", "Wv"))
        Win = sb("Win", [P, KD, 2 * HID])
        Wout = sb("Wout", [P, NH, D])
        place.pop().close()
        x2h, x2l = (sb(n, [P, KD, GT], f32r) for n in ("x2h", "x2l"))
        prodh, prodl = (sb(n, [P, NH, GT], f32r) for n in ("prodh", "prodl"))
        hf = sb("hf", [P, J, D])
        pl = sb("pl", [P, J, 2, ROW])
        emptyrow = pl[0:SP_, :, :, :].rearrange("p j k n -> p (j k n)")[:, 0:SJ * ROW]
        xtT = x2T
        lgs = sb("lgs", [P, J, E])
        oh = sb("oh", [P, J * 2, E])
        ohc = sb("ohc", [P, J * 2, E])
        osum = sb("osum", [P, J, E], bf16)
        oacc = sb("oacc", [P, E], bf16)
        osg = sb("osg", [P, E])
        slot = sb("slot", [P, J * 2], i32)
        tokf = sb("tokf", [P, J * 2])
        m8 = sb("m8", [P, J, 8])
        i8 = sb("i8", [P, J, 8], u32)
        idf = sb("idf", [P, J, 2])
        small = sb("small", [P, 360])
        off = [0]

        def tiny(n):
            off[0] += n
            return small[:, off[0] - n:off[0]]

        st_h, st_2, st_3 = (tiny(24).rearrange("p (j n) -> p j n", j=J) for _ in range(3))
        mv_h, mv_2, mv_3 = (tiny(8).rearrange("p (j n) -> p j n", j=J) for _ in range(3))
        ve_h, r1, va_h, r2, ve_2, r_2, ve_3, r_3, dl, ed, den, wt1 = (tiny(J) for _ in range(12))
        gsum, gvar, grst = (tiny(64) for _ in range(3))
        pos, slf, over = (tiny(J * 2) for _ in range(3))

        place.pop().close()
        place.append(ctx.enter_context(ExitStack()))
        W1 = sb("W1", [P, KD, F])
        W2 = sb("W2", [P, MF, D])
        W1h, W1l = (sb(n, [P, KD, F], f32r) for n in ("W1h", "W1l"))
        W2h, W2l = (sb(n, [P, MF, D], f32r) for n in ("W2h", "W2l"))
        xr = [sb(f"xr{n}", [SP_, SJ, ROW]) for n in range(2)]
        meta = [sb(f"meta{n}", [SP_, SJ, 2]) for n in range(2)]
        xeh, xel = (sb(n, [P, KD, C], f32r) for n in ("xeh", "xel"))
        he = sb("he", [P, 2, C])
        heh, hel = (sb(n, [P, MF, C], f32r) for n in ("heh", "hel"))
        yT = sb("yT", [P, KD, C])
        yw = sb("yw", [SP_, SJ, D])

        bank = [ctx.enter_context(nc.psum_tensor(f"bank{n}", [P, 512], f32)) for n in range(8)]

        in_small, in_w, in_ffn, in_moe, in_empty = (sem(n) for n in ("in_small", "in_w", "in_ffn", "in_moe", "in_empty"))
        consts_set = sem("consts_set")
        strict_set = sem("strict_set")
        passed = sem("passed")
        slots_empty = sem("slots_empty")
        first_idx_in, idx_in, emb_landed = sem("first_idx_in"), sem("idx_in"), sem("emb_landed")
        h_set, stats_h, ve_h_set, va_h_set, r1_set, r2_set, a_set, an_set, abo_set = (
            sem(n) for n in ("h_set", "stats_h", "ve_h_set", "va_h_set", "r1_set", "r2_set", "a_set", "an_set", "abo_set"))
        xT_full, xT_taken = sem("xT_full"), sem("xT_taken")
        qk_full, qk_taken = sem("qk_full"), sem("qk_taken")
        gate_full, gate_taken = sem("gate_full"), sem("gate_taken")
        v_full, v_taken = sem("v_full"), sem("v_taken")
        kt_full, kt_taken = sem("kt_full"), sem("kt_taken")
        kX_set = sem("kX_set")
        sc_full, sc_masked = sem("sc_full"), sem("sc_masked")
        kv_full, kv_added, state_set = sem("kv_full"), sem("kv_added"), sem("state_set")
        ret_full, ret_taken = sem("ret_full"), sem("ret_taken")
        gsum_set, xc_set, sq_set, gvar_set, gve_set, grst_set, gn_set = (
            sem(n) for n in ("gsum_set", "xc_set", "sq_set", "gvar_set", "gve_set", "grst_set", "gn_set"))
        gnT_full, gnT_taken, gg_set = sem("gnT_full"), sem("gnT_taken"), sem("gg_set")
        wo_full, wo_taken = sem("wo_full"), sem("wo_taken")
        stats_2, ve_2_set, r_2_set, x2n_set = (sem(n) for n in ("stats_2", "ve_2_set", "r_2_set", "x2n_set"))
        x2T_full, x2T_taken = sem("x2T_full"), sem("x2T_taken")
        u_full, u_taken, g_full, prod_set = sem("u_full"), sem("u_taken"), sem("g_full"), sem("prod_set")
        winout_high, winout_low = sem("winout_high"), sem("winout_low")
        w_high, w_low, xnl_set, pe_in = sem("w_high"), sem("w_low"), sem("xnl_set"), sem("pe_in")
        x2l_set, prodh_set, prodl_set = sem("x2l_set"), sem("prodh_set"), sem("prodl_set")
        hx_add, hx_set = sem("hx_add"), sem("hx_set")
        o_full, hf_set, out_done = sem("o_full"), sem("hf_set"), sem("out_done")
        stats_3, ve_3_set, r_3_set, xt_set = (sem(n) for n in ("stats_3", "ve_3_set", "r_3_set", "xt_set"))
        xtT_full, xtT_taken = sem("xtT_full"), sem("xtT_taken")
        lg_full, lg_taken = sem("lg_full"), sem("lg_taken")
        top_set, dl_set, ed_set, oh_set, osum_set = (sem(n) for n in ("top_set", "dl_set", "ed_set", "oh_set", "osum_set"))
        route = sem("route")
        cnt_full, cnt_taken = sem("cnt_full"), sem("cnt_taken")
        slot_set, wt_set = sem("slot_set"), sem("wt_set")
        rows_copied, scattered = sem("rows_copied"), sem("scattered")
        bn, bn_3 = sem("bn"), sem("bn_3")
        w1_in, w2_in = sem("w1_in"), sem("w2_in")
        w1h_set, w1l_set = sem("w1h_set"), sem("w1l_set")
        w2h_set, w2l_set, w2l_also = sem("w2h_set"), sem("w2l_set"), sem("w2l_also")
        meta_set = sem("meta_set")
        heh_set, hel_set = sem("heh_set"), sem("hel_set")
        xr_in = [sem(f"xr_in{n}") for n in range(2)]
        xeT_full, xeh_set, xel_set = sem("xeT_full"), sem("xeh_set"), sem("xel_set")
        h1_full, h1_taken = sem("h1_full"), sem("h1_taken")
        y_full, y_taken = sem("y_full"), sem("y_taken")
        yt_full, yt_taken = sem("yt_full"), sem("yt_taken")
        added = sem("added")

        block = ctx.enter_context(nc.Block())

        def wait(eng, s, n):
            if isinstance(n, int) and n <= 0:
                return
            eng.wait_ge(s, n)

        def wait_apart(eng, s, n):
            wait(eng, s, n)
            if not isinstance(n, int):
                eng.sem_inc(passed, 1)

        def own_columns(j, g, n):
            whole = vz[:, j, g * 256:g * 256 + 16]
            return bass.AP(whole.tensor, whole.offset, [list(whole.ap[0]), [256, n], [4 * HD + HD, 4], [1, HD]])

        def steps(eng, step):
            step(0, 0, True, False, True, 0)
            step(1, 1, True, True, True, 0)
            with eng.Fori(0, (G - 4) // 2) as i:
                for r in range(2):
                    step(i * 2 + (2 + r), r, True, True, True, i + 1)
            step(G - 2, 0, True, True, True, G // 2 - 1)
            step(G - 1, 1, True, True, False, G // 2 - 1)
            step(G, 0, False, True, False, G // 2)

        def experts(eng, part):
            part(0, 0, True, False, 1)
            part(1, 1, False, False, 1)
            with eng.Fori(0, (E - 4) // 2) as i:
                for r in range(2):
                    part(i * 2 + (2 + r), r, False, False, i + 2)
            part(E - 2, 0, False, False, E // 2)
            part(E - 1, 1, False, True, E // 2)

        @block.sync
        def _(sp):
            sp.dma_start(idxg[:, :], idx[0]).then_inc(first_idx_in, 16)
            sp.dma_start(pe_tab[:, :, :], positions[0]).then_inc(pe_in, 16)
            sp.dma_start(const[:, :], consts).then_inc(in_small, 16)
            sp.dma_start(vec[:, :], vecs).then_inc(in_small, 16)
            sp.dma_start(row[:, :, :], rows.partition_broadcast(P)).then_inc(in_small, 16)
            sp.dma_start(gb[:, :], gate_b.partition_broadcast(P)).then_inc(in_small, 16)
            sp.dma_start(Gw[:, :, :], gate_w.rearrange("(k p) n -> p k n", p=P)).then_inc(in_small, 16)
            sp.wait_ge(emb_landed, 16 * J)
            for dst, src in ((Wq, wq), (Wk, wk), (Wg, wg), (Wv, wv), (Wo, wo)):
                sp.dma_start(dst[:, :, :], src.rearrange("(k p) n -> p k n", p=P)).then_inc(in_w, 16)
            sp.wait_ge(h_set, 1)
            sp.dma_start(pe_tab[:, :, :], positions[1]).then_inc(pe_in, 16)
            sp.dma_start(Win[:, :, :], w_in.rearrange("(k p) n -> p k n", p=P)).then_inc(in_ffn, 16)
            full = HID // P
            sp.dma_start(Wout[:, 0:full, :], w_out[0:full * P, :].rearrange("(k p) n -> p k n", p=P)).then_inc(in_ffn, 16)
            sp.dma_start(Wout[0:HID - full * P, full, :], w_out[full * P:HID, :]).then_inc(in_ffn, 16)
            sp.dma_start(emptyrow, empty.rearrange("p j n -> p (j n)")).then_inc(in_empty, 16)
            sp.dma_start(B1[:, :, :], b1).then_inc(in_moe, 16)
            sp.dma_start(B2[:, :, :], b2).then_inc(in_moe, 16)

            sp.wait_ge(emb_landed, 16 * 2 * J)
            sp.wait_ge(in_empty, 16)
            sp.dma_start(xe.rearrange("(e p j) n -> p e (j n)", e=E, p=SP_),
                         emptyrow.unsqueeze(1).to_broadcast([SP_, E, SJ * ROW])).then_inc(slots_empty, 16)
            sp.dma_start(out[T:T + DUMP, :].rearrange("(p j) d -> p (j d)", p=SP_), emptyrow[:, 0:SJ * D]).then_inc(slots_empty, 16)

            out_g = out[0:T, :].rearrange("(g j p) d -> g p j d", j=J, p=P)

            def step(s, par, first, second, ahead, seq):
                if not first:
                    wait(sp, v_full, 2 * G)
                    sp.dma_start(W1[:, :, :], w1[0]).then_inc(w1_in, 16)
                    wait(sp, sc_full, 16 * G)
                    wait(sp, wo_full, 2 * G)
                    sp.dma_start(W2[:, :, :], w2[0]).then_inc(w2_in, 16)
                if second:
                    wait(sp, hf_set, 2 * s)
                    sp.dma_start(out_g[s - 1], hf[:, :, :]).then_inc(out_done, 16)
                if not isinstance(s, int) or s + 2 < G:
                    wait(sp, h_set, s + 2)
                    sp.dma_start(pe_tab[:, :, :], positions[par]).then_inc(pe_in, 16)
            steps(sp, step)

            sp.wait_ge(scattered, 16 * 2 * J * G)
            xe_e = xe.rearrange("(e j p) n -> e p j n", e=E, p=SP_)

            def part(e, b, first, last, n):
                if first:
                    sp.dma_start(xr[0][:, :, :], xe_e[0]).then_inc(xr_in[0], 16)
                if last:
                    return
                if not first:
                    wait(sp, xeT_full, KD * e)
                    wait(sp, meta_set, e)
                sp.dma_start(xr[1 - b][:, :, :], xe_e[e + 1]).then_inc(xr_in[1 - b], 16)
                wait(sp, w1l_set, KD * (e + 1))
                sp.dma_start(W1[:, :, :], w1[e + 1]).then_inc(w1_in, 16)
                wait(sp, w2l_set, e + 1)
                wait(sp, w2l_also, e + 1)
                sp.dma_start(W2[:, :, :], w2[e + 1]).then_inc(w2_in, 16)
            experts(sp, part)
            sp.wait_ge(out_done, 16 * G)

        @block.gpsimd
        def _(pool):
            def gather(g, par):
                if isinstance(g, int) and g == 0:
                    pool.wait_ge(first_idx_in, 16)
                else:
                    wait_apart(pool, idx_in, 16 * g)
                for j in range(J):
                    pool.indirect_dma_start(hres[par][:, j, :], None, emb,
                                            bass.IndirectOffsetOnAxis(ap=idxg[:, j:j + 1], axis=0)).then_inc(emb_landed, 16)

            def head(g, par):
                wait_apart(pool, emb_landed, 16 * J * (g + 1))
                if not isinstance(g, int) or g < G - 1:
                    pool.dma_start(idxg[:, :], idx[g + 1]).then_inc(idx_in, 16)
                wait_apart(pool, pe_in, 16 * (g + 1))
                pool.tensor_tensor(hres[par][:, :, :], hres[par][:, :, :], pe_tab[:, :, :],
                                   ALU.add).then_inc(h_set, 1)

            def head_roots(g, par):
                wait_apart(pool, stats_h, g + 1)
                pool.tensor_scalar(ve_h, mv_h[:, :, 1], EPS, None, ALU.add).then_inc(ve_h_set, 1)
                wait_apart(pool, ve_h_set, g + 1)
                pool.tensor_tensor(r1, ve_h, half[:, 0:J], ALU.pow).then_inc(r1_set, 1)
                wait_apart(pool, r1_set, g + 1)
                pool.tensor_tensor(va_h, r1, r1, ALU.mult).then_inc(va_h_set, 1)
                wait_apart(pool, va_h_set, 3 * g + 1)
                pool.tensor_tensor(va_h, va_h, mv_h[:, :, 1], ALU.mult).then_inc(va_h_set, 1)
                wait_apart(pool, va_h_set, 3 * g + 2)
                pool.tensor_scalar(va_h, va_h, EPS, None, ALU.add).then_inc(va_h_set, 1)
                wait_apart(pool, va_h_set, 3 * g + 3)
                pool.tensor_tensor(r2, va_h, half[:, 0:J], ALU.pow).then_inc(r2_set, 1)

            def a_plus_bo(g, par):
                wait_apart(pool, an_set, g + 1)
                pool.tensor_tensor(a[par][:, :, :], a[par][:, :, :],
                                   row[:, 1, :].unsqueeze(1).to_broadcast([P, J, D]), ALU.add).then_inc(abo_set, 1)

            gather(0, 0)
            pool.memset(half[:, :], -0.5).then_inc(consts_set, 1)
            pool.memset(euler[:, :], float(np.e)).then_inc(consts_set, 1)
            pool.memset(ones[:, :], 1.0).then_inc(consts_set, 1)
            pool.memset(oacc[:, :], 0.0).then_inc(consts_set, 1)
            pool.wait_ge(consts_set, 4)
            pool.wait_ge(in_small, 16 * 5)
            head(0, 0)
            head_roots(0, 0)
            gather(1, 1)
            a_plus_bo(0, 0)

            def scatter(s):
                if isinstance(s, int) and s < 2:
                    return
                pool.wait_ge(slots_empty, 32)
                wait_apart(pool, rows_copied, s - 1)
                wait_apart(pool, slot_set, s - 1)
                wait_apart(pool, wt_set, s - 1)
                for j in range(J):
                    for k in range(2):
                        pool.indirect_dma_start(
                            xe, bass.IndirectOffsetOnAxis(ap=slot[:, 2 * j + k:2 * j + k + 1], axis=0),
                            pl[:, j, k, :], None, bounds_check=E * CP - 1, oob_is_err=False).then_inc(scattered, 16)

            def step(s, par, first, second, ahead, seq):
                p = s - 1
                if second:
                    wait_apart(pool, wo_taken, 2 * s)
                    wait_apart(pool, out_done, 16 * p)
                    wait_apart(pool, xt_set, 2 * p)
                    pool.tensor_tensor(hf[:, :, :], hres[1 - par][:, :, :], a[1 - par][:, :, :], ALU.add).then_inc(hx_add, 1)
                    wait_apart(pool, hx_add, s)
                    pool.tensor_tensor(hf[:, :, :], hf[:, :, :], row[:, 2, :].unsqueeze(1).to_broadcast([P, J, D]),
                                       ALU.add).then_inc(hx_set, 1)
                    if ahead:
                        gather(s + 1, 1 - par)
                scatter(s)
                if ahead:
                    head(s + 1, 1 - par)
                    head_roots(s + 1, 1 - par)
                if first:
                    for n, (lo, hi) in enumerate(HEADS_NORMED):
                        wait_apart(pool, gvar_set, NN * s + n + 1)
                        gv = gvar[:, H * lo:H * hi]
                        pool.tensor_scalar(gv, gv, 1.0 / HD, EPS, ALU.mult, ALU.add).then_inc(gve_set, 1)
                        wait_apart(pool, gve_set, NN * s + n + 1)
                        pool.tensor_tensor(grst[:, H * lo:H * hi], gv, half[:, 0:H * (hi - lo)], ALU.pow).then_inc(grst_set, 1)
                if second:
                    for i in range(2):
                        v, t = ve_3[:, 2 * i:2 * i + 2], 2 * p + i + 1
                        wait_apart(pool, stats_3, t)
                        pool.tensor_scalar(v, mv_3[:, 2 * i:2 * i + 2, 1], EPS, None, ALU.add).then_inc(ve_3_set, 1)
                        wait_apart(pool, ve_3_set, t)
                        pool.tensor_tensor(r_3[:, 2 * i:2 * i + 2], v, half[:, 0:2], ALU.pow).then_inc(r_3_set, 1)
                if first:
                    wait_apart(pool, stats_2, s + 1)
                    pool.tensor_scalar(ve_2, mv_2[:, :, 1], EPS, None, ALU.add).then_inc(ve_2_set, 1)
                    wait_apart(pool, ve_2_set, s + 1)
                    pool.tensor_tensor(r_2, ve_2, half[:, 0:J], ALU.pow).then_inc(r_2_set, 1)
                if second:
                    wait_apart(pool, dl_set, s)
                    pool.tensor_tensor(ed, euler[:, :], dl, ALU.pow).then_inc(ed_set, 1)
                if ahead:
                    a_plus_bo(s + 1, 1 - par)
            steps(pool, step)
            scatter(G + 1)

            def w2_low(e):
                wait_apart(pool, w2h_set, KD * (e + 1))
                t = slice(MF // 2, MF)
                pool.tensor_tensor(W2l[:, t, :], W2[:, t, :], W2h[:, t, :].bitcast(f32), ALU.subtract).then_inc(w2l_also, 1)

            def part(e, b, first, last, n):
                if first:
                    w2_low(0)
                    pool.wait_ge(out_done, 16 * G)
                wait_apart(pool, xr_in[b], 16 * n)
                wait_apart(pool, added, 16 * SJ * e)
                pool.tensor_copy(meta[b][:, :, :], xr[b][:, :, D:ROW]).then_inc(meta_set, 1)
                if not last:
                    w2_low(e + 1)
                wait_apart(pool, meta_set, e + 1)
                wait_apart(pool, yt_taken, SJ * (e + 1))
                for j in range(SJ):
                    pool.indirect_dma_start(
                        out, bass.IndirectOffsetOnAxis(ap=meta[b][0:SR[j], j, 0:1].bitcast(i32), axis=0),
                        yw[0:SR[j], j, :], None, compute_op=ALU.add).then_inc(added, 16)
            experts(pool, part)
            pool.wait_ge(added, 16 * SJ * E)

        @block.scalar
        def _(act):
            act.wait_ge(in_small, 16 * 5)

            def vcol(n):
                return vec[:, n:n + 1]

            def normed(g, par):
                wait(act, a_set, g + 1)
                wait(act, r2_set, g + 1)
                for j in range(J):
                    last = act.activation(an[:, j, :], a[par][:, j, :], ACT.Copy, scale=r2[:, j:j + 1])
                last.then_inc(an_set, 1)

            def xT(g):
                for k in range(KD):
                    wait(act, xT_full, KD * g + k + 1)
                    for xn in (xnT, xnh):
                        last = act.activation(xn[:, k, :], bank[6 + k][:, :], ACT.Identity,
                                              scale=vcol(V_N1W + k), bias=vcol(V_N1B + k))
                    last.then_inc(xT_taken, 1)

            act.wait_ge(in_w, 16 * 5)
            for high, raw in ((Wqh, Wq), (Wkh, Wk), (Wgh, Wg), (Wvh, Wv)):
                act.activation(high[:, :, :], raw[:, :, :], ACT.Copy).then_inc(w_high, 1)
            normed(0, 0)
            xT(0)

            def step(s, par, first, second, ahead, seq):
                p = s - 1

                def u(j):
                    if not second:
                        return
                    wait(act, u_full, NH * p + j + 1)
                    wait(act, prodl_set, NH * p + max(j - 1, 0))
                    w = HW[j]
                    act.activation(su[0:w, j % 2, :], bank[4][0:w, :], ACT.Silu,
                                   bias=vec[0:w, V_BU + j:V_BU + j + 1]).then_inc(u_taken, 1)

                def take_ret(c):
                    if not first:
                        return
                    wait(act, ret_full, J * s + c + 1)
                    if c == 0:
                        wait(act, gn_set, NN * s)
                    act.activation(ret[:, c, :], bank[6][:, 0:D], ACT.Copy).then_inc(ret_taken, 1)

                def squares(n):
                    if not first:
                        return
                    lo, hi = HEADS_NORMED[n]
                    wait(act, xc_set, NN * s + n + 1)
                    wait(act, gvar_set, NN * s + n)
                    act.activation(sq[:, 0:hi - lo, :], ret[:, lo:hi, :], ACT.Square).then_inc(sq_set, 1)

                if second:
                    for k in range(KD):
                        wait(act, x2T_full, KD * p + k + 1)
                        if k == 0:
                            wait(act, lg_full, p)
                        for x2 in (x2T, x2h):
                            last = act.activation(x2[:, k, :], bank[6 + k][:, :], ACT.Identity,
                                                  scale=vcol(V_N2W + k), bias=vcol(V_N2B + k))
                        last.then_inc(x2T_taken, 1)

                def keys(c):
                    if not first:
                        return
                    if c > 1:
                        wait(act, sc_full, 16 * s + 4 * (c - 1))
                    for o in range(4):
                        act.activation(kX[:, c % 2, o, :, :], kT[:, :, c * P:(c + 1) * P], ACT.Copy,
                                       scale=const[:, K_PAR + o:K_PAR + o + 1]).then_inc(kX_set, 1)

                if first:
                    wait(act, gg_set, 2 * s)
                    for m in range(KD):
                        wait(act, gate_full, KD * s + m + 1)
                        act.activation(gateT[:, m, :], bank[4 + m][:, :], ACT.Silu, bias=vcol(V_BG + m)).then_inc(gate_taken, 1)
                    wait(act, qk_taken, 4 * s + 4)
                    keys(0)
                    keys(1)
                    for i in range(2):
                        wait(act, kt_full, 2 * s + i + 1)
                        act.activation(ktok[:, 2 * i:2 * i + 2, :],
                                       bank[2 + i][:, :].rearrange("p (j d) -> p j d", j=2), ACT.Copy).then_inc(kt_taken, 1)
                u(0)
                u(1)
                keys(2)
                take_ret(0)
                keys(3)
                u(2)
                take_ret(1)
                u(3)
                squares(0)
                take_ret(2)
                squares(1)
                take_ret(3)
                if not second:
                    squares(2)
                if not second:
                    act.wait_ge(in_ffn, 48)
                    for k in range(KD):
                        act.activation(Winh[:, k, :], Win[:, k, :], ACT.Copy).then_inc(winout_high, 1)
                    act.activation(Wouth[:, 0:NH - 1, :], Wout[:, 0:NH - 1, :], ACT.Copy).then_inc(winout_high, 1)
                    act.activation(Wouth[0:HW[-1], NH - 1, :], Wout[0:HW[-1], NH - 1, :], ACT.Copy).then_inc(winout_high, 1)
                u(4)
                if second:
                    squares(2)
                u(5)
                if first:
                    for m in range(KD):
                        wait(act, gnT_full, KD * s + m + 1)
                        act.activation(gnT[:, m, :], bank[m][:, :], ACT.Identity,
                                       scale=vcol(V_GNW + m), bias=vcol(V_GNB + m)).then_inc(gnT_taken, 1)
                if ahead:
                    normed(s + 1, 1 - par)
                    xT(s + 1)
                if second:
                    wait(act, x2l_set, KD * s)
                    for k in range(KD):
                        wait(act, xtT_full, KD * p + k + 1)
                        act.activation(xtT[:, k, :], bank[4 + k][:, :], ACT.Copy).then_inc(xtT_taken, 1)
                    wait(act, xt_set, 2 * s)
                    act.activation(pl[:, :, 1, 0:D], pl[:, :, 0, 0:D], ACT.Copy).then_inc(rows_copied, 1)
            steps(act, step)

            act.wait_ge(in_moe, 32)

            def part(e, b, first, last, n):
                def xe_high(e):
                    for k in range(KD):
                        wait(act, xeT_full, KD * e + k + 1)
                        act.activation(xeh[:, k, :], bank[4 + k][:, 0:C], ACT.Copy).then_inc(xeh_set, 1)

                def w1_high(e):
                    wait(act, w1_in, 16 * (e + 1))
                    wait(act, h1_full, MF * e)
                    for k in range(KD):
                        act.activation(W1h[:, k, :], W1[:, k, :], ACT.Copy).then_inc(w1h_set, 1)

                def w2_high(e, k):
                    if k == 0:
                        wait(act, w2_in, 16 * (e + 1))
                        wait(act, y_full, KD * e)
                    act.activation(W2h[:, 4 * k:4 * k + 4, :], W2[:, 4 * k:4 * k + 4, :], ACT.Copy).then_inc(w2h_set, 1)

                def weighted(e, b):
                    wait(act, added, 16 * SJ * e)
                    wait(act, meta_set, e + 1)
                    for j in range(SJ):
                        wait(act, yt_full, SJ * e + max(j + 1, 2))
                        act.activation(yw[0:SR[j], j, :], bank[4 + j // 2][0:SR[j], (j % 2) * D:(j % 2 + 1) * D], ACT.Copy,
                                       scale=meta[b][0:SR[j], j, 1:2]).then_inc(yt_taken, 1)

                if first:
                    w1_high(0)
                    xe_high(0)
                for m in range(MF):
                    wait(act, h1_full, MF * e + m + 1)
                    wait(act, hel_set, MF * e + m - 1 if m > 1 or not first else 0)
                    act.activation(he[:, m % 2, :], bank[m % 4][:, 0:C], ACT.Gelu,
                                   bias=B1_col(e, m)).then_inc(h1_taken, 1)
                    if m == 0 or m == 2:
                        w2_high(e, m // 2)
                    if m == 4 and not first:
                        weighted(e - 1, 1 - b)
                if not last:
                    w1_high(e + 1)
                    xe_high(e + 1)
                else:
                    weighted(e, b)

            def B1_col(e, m):
                return B1[:, :, :].rearrange("p e m -> p (e m)")[:, bass.ds(e * MF + m, 1)]
            experts(act, part)

        @block.vector
        def _(dve):
            dve.memset(vz[:, :, :], 0.0).then_inc(strict_set, 1)
            dve.wait_ge(in_small, 16 * 5)
            dve.tensor_copy(strict[:, :], const[:, K_STRICT:K_IOTA]).then_inc(strict_set, 1)
            dve.tensor_copy(tokf[:, :], tok0).then_inc(strict_set, 1)
            dve.wait_ge(consts_set, 4)

            def stats(x, st, mv, done, n_bn):
                for j in range(J):
                    last = dve.bn_stats(st[:, j, :], x[:, j, :])
                last.then_inc(bn, 1)
                wait_apart(dve, bn, n_bn)
                for j in range(J):
                    last = dve.bn_aggr(mv[:, j, :], st[:, j, :])
                last.then_inc(done, 1)

            def bn_count(s, ahead, which):
                n = 1 + 2 * s
                return n + ahead + which

            def head_stats(g, par, n_bn):
                wait(dve, h_set, g + 1)
                stats(hres[par], st_h, mv_h, stats_h, n_bn)

            def head_norm(g, par):
                wait(dve, r1_set, g + 1)
                wait(dve, hx_add, g - 1)
                for j in range(J):
                    last = dve.tensor_scalar(a[par][:, j, :], hres[par][:, j, :], mv_h[:, j, 0:1], r1[:, j:j + 1],
                                             ALU.subtract, ALU.mult)
                last.then_inc(a_set, 1)

            head_stats(0, 0, 1)
            head_norm(0, 0)
            for n, (low, raw, high) in enumerate(((Wql, Wq, Wqh), (Wkl, Wk, Wkh), (Wgl, Wg, Wgh), (Wvl, Wv, Wvh))):
                dve.wait_ge(w_high, n + 1)
                dve.tensor_tensor(low[:, :, :], raw[:, :, :], high[:, :, :].bitcast(f32), ALU.subtract).then_inc(w_low, 1)

            def xn_low(g):
                for k in range(KD):
                    wait(dve, xT_taken, KD * g + k + 1)
                    dve.tensor_tensor(xnl[:, k, :], xnT[:, k, :], xnh[:, k, :].bitcast(f32), ALU.subtract).then_inc(xnl_set, 1)

            xn_low(0)

            def place_rows(s):
                if isinstance(s, int) and s < 2:
                    return
                q = s - 2
                wait(dve, cnt_full, q + 1)
                dve.tensor_tensor(ohc[:, :, :].rearrange("p (j k) e -> p j k e", k=2),
                                  bank[5][:, 0:J * E].rearrange("p (j e) -> p j e", j=J).unsqueeze(2).to_broadcast([P, J, 2, E]),
                                  oh[:, :, :].rearrange("p (j k) e -> p j k e", k=2), ALU.mult).then_inc(cnt_taken, 1)
                dve.tensor_reduce(osg[:, :], osum[:, :, :].rearrange("p j e -> p e j"), AX.X, ALU.add).then_inc(route, 1)
                dve.wait_ge(cnt_taken, q + 1)
                dve.tensor_reduce(pos, ohc[:, :, :], AX.X, ALU.add).then_inc(route, 1)
                dve.wait_ge(route, 8 * q + 5)
                dve.tensor_tensor(oacc[:, :], oacc[:, :], osg[:, :], ALU.add).then_inc(route, 1)
                dve.scalar_tensor_tensor(slf, idf[:, :, :].rearrange("p j k -> p (j k)"), float(CP), pos,
                                         ALU.mult, ALU.add).then_inc(route, 1)
                dve.tensor_scalar(over, pos, float(C), 1e6, ALU.is_ge, ALU.mult).then_inc(route, 1)
                dve.wait_ge(route, 8 * q + 8)
                dve.tensor_tensor(slot[:, :], slf, over, ALU.add).then_inc(slot_set, 1)

            def step(s, par, first, second, ahead, seq):
                p = s - 1

                def glu(j):
                    if not second:
                        return
                    w = HW[j]
                    wait(dve, g_full, NH * p + j + 1)
                    wait(dve, u_taken, NH * p + j + 1)
                    dve.scalar_tensor_tensor(su[0:w, j % 2, :], bank[5][0:w, :], vec[0:w, V_BGL + j:V_BGL + j + 1],
                                             su[0:w, j % 2, :], ALU.add, ALU.mult).then_inc(prod_set, 1)

                def split(j):
                    if not second:
                        return
                    w = HW[j]
                    wait(dve, prod_set, NH * p + j + 1)
                    dve.tensor_copy(prodh[0:w, j, :], su[0:w, j % 2, :]).then_inc(prodh_set, 1)
                    wait(dve, prodh_set, NH * p + j + 1)
                    dve.tensor_tensor(prodl[0:w, j, :], su[0:w, j % 2, :], prodh[0:w, j, :].bitcast(f32),
                                      ALU.subtract).then_inc(prodl_set, 1)

                def mask(c):
                    if not first:
                        return
                    for q in range(4):
                        wait(dve, sc_full, 16 * s + 4 * c + q + 1)
                        dve.tensor_tensor(sm[:, q, :, :], bank[q][:, :].rearrange("p (h n) -> p h n", h=4),
                                          causal.unsqueeze(1).to_broadcast([P, 4, P]), ALU.mult).then_inc(sc_masked, 1)

                def next_state(c):
                    if not first:
                        return
                    wait(dve, kv_full, J * s + c + 1)
                    if par == 0 and c == 0:
                        dve.tensor_tensor(state[:, :], bank[7][:, 0:D], bd_tab, ALU.mult).then_inc(state_set, 1)
                        return
                    dve.tensor_tensor(stmp[:, :], bank[7][:, 0:D], state[:, :], ALU.add).then_inc(kv_added, 1)
                    dve.wait_ge(kv_added, seq * 7 + (4 * par + c))
                    dve.tensor_tensor(state[:, :], stmp[:, :], bd_tab, ALU.mult).then_inc(state_set, 1)

                def gn_mean(n):
                    if not first:
                        return
                    lo, hi = HEADS_NORMED[n]
                    r4 = ret[:, lo:hi, :].rearrange("p j (h d) -> p (j h) d", h=H)
                    gs = gsum[:, H * lo:H * hi]
                    wait(dve, ret_taken, J * s + hi)
                    dve.tensor_reduce(gs, r4, AX.X, ALU.add).then_inc(gsum_set, 1)
                    wait(dve, gsum_set, NN * s + n + 1)
                    dve.scalar_tensor_tensor(r4, gs.unsqueeze(2).to_broadcast([P, H * (hi - lo), HD]), -1.0 / HD, r4,
                                             ALU.mult, ALU.add).then_inc(xc_set, 1)

                def gn_var(n):
                    if not first:
                        return
                    lo, hi = HEADS_NORMED[n]
                    wait(dve, sq_set, NN * s + n + 1)
                    if n == 0:
                        wait(dve, grst_set, NN * s)
                    dve.tensor_reduce(gvar[:, H * lo:H * hi],
                                      sq[:, 0:hi - lo, :].rearrange("p j (h d) -> p (j h) d", h=H), AX.X, ALU.add).then_inc(gvar_set, 1)

                if first:
                    place_rows(s)
                    for n in range(4):
                        w, m = n // 2, n % 2
                        wait(dve, qk_full, 4 * s + n + 1)
                        dve.scalar_tensor_tensor(
                            (qT, kT)[w][:, m, :].rearrange("p (j n) -> p j n", j=J),
                            bank[n][:, :].rearrange("p (j n) -> p j n", j=J),
                            vec[:, (V_BQ, V_BK)[w] + m:(V_BQ, V_BK)[w] + m + 1],
                            (q_tab, k_tab)[w][:, m, :].unsqueeze(1).to_broadcast([P, J, P]),
                            ALU.add, ALU.mult).then_inc(qk_taken, 1)
                if second:
                    for k in range(KD):
                        wait(dve, x2T_taken, KD * p + k + 1)
                        dve.tensor_tensor(x2l[:, k, :], x2T[:, k, :], x2h[:, k, :].bitcast(f32), ALU.subtract).then_inc(x2l_set, 1)
                if not first:
                    place_rows(s)
                if first:
                    for i in range(2):
                        wait(dve, v_full, 2 * s + i + 1)
                        for jj in range(2):
                            last = dve.tensor_tensor(own_columns(2 * i + jj, 0, 4),
                                                     bank[i][:, jj * D:(jj + 1) * D].rearrange("p (g r d) -> p g r d", g=4, r=4),
                                                     row[:, 0, :].rearrange("p (g r d) -> p g r d", g=4, r=4), ALU.add)
                        last.then_inc(v_taken, 1)
                glu(0)
                mask(0)
                split(0)
                glu(1)
                if ahead:
                    head_stats(s + 1, 1 - par, bn_count(s, ahead, 0))
                next_state(0)
                mask(1)
                split(1)
                glu(2)
                next_state(1)
                mask(2)
                split(2)
                glu(3)
                gn_mean(0)
                next_state(2)
                gn_var(0)
                mask(3)
                gn_mean(1)
                split(3)
                next_state(3)
                gn_var(1)
                gn_mean(2)
                gn_var(2)
                if not second:
                    for n, (low, raw, high) in enumerate([(Winl[:, k, :], Win[:, k, :], Winh[:, k, :]) for k in range(KD)] + [
                            (Woutl[:, 0:NH - 1, :], Wout[:, 0:NH - 1, :], Wouth[:, 0:NH - 1, :]),
                            (Woutl[0:HW[-1], NH - 1, :], Wout[0:HW[-1], NH - 1, :], Wouth[0:HW[-1], NH - 1, :])]):
                        dve.wait_ge(winout_high, n + 1)
                        dve.tensor_tensor(low, raw, high.bitcast(f32), ALU.subtract).then_inc(winout_low, 1)
                glu(4)
                split(4)
                glu(5)
                split(5)
                if first:
                    for n, (lo, hi) in enumerate(HEADS_NORMED):
                        wait(dve, grst_set, NN * s + n + 1)
                        dve.tensor_tensor(gn[:, lo:hi, :].rearrange("p j (h d) -> p (j h) d", h=H),
                                          ret[:, lo:hi, :].rearrange("p j (h d) -> p (j h) d", h=H),
                                          grst[:, H * lo:H * hi].unsqueeze(2).to_broadcast([P, H * (hi - lo), HD]),
                                          ALU.mult).then_inc(gn_set, 1)
                def gated():
                    if not first:
                        return
                    for m in range(KD):
                        wait(dve, gnT_taken, KD * s + m + 1)
                        dve.tensor_tensor(gnT[:, m, :], gnT[:, m, :], gateT[:, m, :], ALU.mult).then_inc(gg_set, 1)

                def next_rows(i):
                    wait(dve, r_3_set, 2 * p + i + 1)
                    if i == 0:
                        dve.wait_ge(slots_empty, 32)
                        wait(dve, scattered, 16 * 2 * J * p)
                    for j in (2 * i, 2 * i + 1):
                        last = dve.tensor_scalar(pl[:, j, 0, 0:D], hf[:, j, :], mv_3[:, j, 0:1], r_3[:, j:j + 1],
                                                 ALU.subtract, ALU.mult)
                    last.then_inc(xt_set, 1)

                def next_input():
                    if ahead:
                        head_norm(s + 1, 1 - par)

                if not second:
                    next_input()
                    gated()
                if second:
                    wait(dve, hx_set, s)
                    for i in range(2):
                        wait(dve, o_full, 2 * p + i + 1)
                        dve.tensor_tensor(hf[:, 2 * i:2 * i + 2, :], bank[4 + i][:, :].rearrange("p (j d) -> p j d", j=2),
                                          hf[:, 2 * i:2 * i + 2, :], ALU.add).then_inc(hf_set, 1)
                        dve.wait_ge(hf_set, 2 * p + i + 1)
                        for j in (2 * i, 2 * i + 1):
                            last = dve.bn_stats(st_3[:, j, :], hf[:, j, :])
                        last.then_inc(bn_3, 1)
                        wait_apart(dve, bn_3, 2 * p + i + 1)
                        for j in (2 * i, 2 * i + 1):
                            last = dve.bn_aggr(mv_3[:, j, :], st_3[:, j, :])
                        last.then_inc(stats_3, 1)
                        if i == 0:
                            next_input()
                            gated()
                        else:
                            next_rows(0)
                            next_rows(1)
                def residual(i):
                    if not first:
                        return
                    if i == 0:
                        wait(dve, abo_set, s + 1)
                    wait(dve, wo_full, 2 * s + i + 1)
                    dve.tensor_tensor(a[par][:, 2 * i:2 * i + 2, :], bank[2 + i][:, :].rearrange("p (j d) -> p j d", j=2),
                                      a[par][:, 2 * i:2 * i + 2, :], ALU.add).then_inc(wo_taken, 1)
                if ahead:
                    xn_low(s + 1)
                residual(0)
                residual(1)
                if first:
                    wait(dve, wo_taken, 2 * s + 2)
                    stats(a[par], st_2, mv_2, stats_2, bn_count(s, ahead, 1))
                def second_input():
                    wait(dve, r_2_set, s + 1)
                    if ahead:
                        wait(dve, xT_full, KD * (s + 2))
                    for j in range(J):
                        last = dve.tensor_scalar(x2n[:, j, :], a[par][:, j, :], mv_2[:, j, 0:1], r_2[:, j:j + 1],
                                                 ALU.subtract, ALU.mult)
                    last.then_inc(x2n_set, 1)
                if first and not ahead:
                    second_input()
                if second:
                    wait(dve, lg_full, s)
                    dve.tensor_tensor(lgs[:, :, :], bank[4][:, 0:J * E].rearrange("p (j e) -> p j e", j=J),
                                      gb[:, :].unsqueeze(1).to_broadcast([P, J, E]), ALU.add).then_inc(lg_taken, 1)
                    wait_apart(dve, lg_taken, s)
                    for j in range(J):
                        last = dve.max(m8[:, j, :], lgs[:, j, :])
                    last.then_inc(top_set, 1)
                    wait(dve, top_set, 2 * p + 1)
                    dve.tensor_tensor(dl, m8[:, :, 1], m8[:, :, 0], ALU.subtract).then_inc(dl_set, 1)
                    for j in range(J):
                        last = dve.max_index(i8[:, j, :], m8[:, j, :], lgs[:, j, :])
                    last.then_inc(top_set, 1)
                    wait(dve, top_set, 2 * p + 2)
                    dve.tensor_copy(idf[:, :, :], i8[:, :, 0:2]).then_inc(route, 1)
                    dve.wait_ge(route, 8 * p + 1)
                    dve.tensor_tensor(oh[:, :, :], iota.unsqueeze(1).to_broadcast([P, J * 2, E]),
                                      idf[:, :, :].rearrange("p j k -> p (j k)").unsqueeze(2).to_broadcast([P, J * 2, E]),
                                      ALU.is_equal).then_inc(oh_set, 1)
                    wait(dve, oh_set, s)
                    o4 = oh[:, :, :].rearrange("p (j k) e -> p j k e", k=2)
                    dve.tensor_tensor(osum[:, :, :], o4[:, :, 0, :], o4[:, :, 1, :], ALU.add).then_inc(osum_set, 1)
                if first and ahead:
                    second_input()
                if second:
                    wait(dve, ed_set, s)
                    dve.tensor_scalar(den, ed, 1.0, None, ALU.add).then_inc(route, 1)
                    dve.wait_ge(route, 8 * p + 2)
                    dve.reciprocal(wt1, den).then_inc(route, 1)
                    dve.wait_ge(route, 8 * p + 3)
                    dve.tensor_copy(pl[:, :, 0, D + 1], wt1)
                    dve.tensor_tensor(pl[:, :, 1, D + 1], ed, wt1, ALU.mult)
                    dve.tensor_copy(pl[:, :, :, D].bitcast(i32), tokf[:, :].rearrange("p (j k) -> p j k", k=2)).then_inc(wt_set, 1)
                    wait(dve, wt_set, s)
                    dve.tensor_scalar(tokf[:, :], tokf[:, :], float(GT), None, ALU.add)

            steps(dve, step)
            place_rows(G + 1)

            def part(e, b, first, last, n):
                def xe_low(e):
                    for k in range(KD):
                        wait(dve, xeh_set, KD * e + k + 1)
                        dve.tensor_tensor(xel[:, k, :], bank[4 + k][:, 0:C], xeh[:, k, :].bitcast(f32),
                                          ALU.subtract).then_inc(xel_set, 1)

                def w1_low(e):
                    for k in range(KD):
                        wait(dve, w1h_set, KD * e + k + 1)
                        dve.tensor_tensor(W1l[:, k, :], W1[:, k, :], W1h[:, k, :].bitcast(f32),
                                          ALU.subtract).then_inc(w1l_set, 1)

                def w2_low(e):
                    wait(dve, w2h_set, KD * e + 1)
                    t = slice(0, MF // 2)
                    dve.tensor_tensor(W2l[:, t, :], W2[:, t, :], W2h[:, t, :].bitcast(f32), ALU.subtract).then_inc(w2l_set, 1)

                if first:
                    w1_low(0)
                    xe_low(0)
                for m in range(MF):
                    wait(dve, h1_taken, MF * e + m + 1)
                    dve.tensor_copy(heh[:, m, :], he[:, m % 2, :]).then_inc(heh_set, 1)
                    wait(dve, heh_set, MF * e + m + 1)
                    dve.tensor_tensor(hel[:, m, :], he[:, m % 2, :], heh[:, m, :].bitcast(f32), ALU.subtract).then_inc(hel_set, 1)
                    if m == 2:
                        w2_low(e)
                if not last:
                    w1_low(e + 1)
                for k in range(KD):
                    if k == 1 and not last:
                        xe_low(e + 1)
                    wait(dve, y_full, KD * e + k + 1)
                    if k == 0:
                        wait(dve, yt_full, SJ * e)
                    dve.tensor_scalar(yT[:, k, :], bank[6 + k][:, 0:C],
                                      B2[:, :, :].rearrange("p e k -> p (e k)")[:, bass.ds(e * KD + k, 1)], None,
                                      ALU.add).then_inc(y_taken, 1)
            dve.wait_ge(in_moe, 32)
            experts(dve, part)

        @block.tensor
        def _(pe):
            pe.wait_ge(in_small, 16 * 5)
            pe.wait_ge(strict_set, 3)
            pe.wait_ge(consts_set, 4)

            def mm(o, l, r, start, stop, loose=False):
                return pe.matmul(o, l, r, start=start, stop=stop, skip_group_check=loose)

            def xT(g):
                wait(pe, an_set, g + 1)
                wait(pe, ret_taken, J * g)
                wait(pe, state_set, J * g)
                for k in range(KD):
                    for j in range(J):
                        last = pe.transpose(bank[6 + k][:, j * P:(j + 1) * P], an[:, j, k * P:(k + 1) * P], ident)
                    last.then_inc(xT_full, 1)

            xT(0)
            pe.wait_ge(in_w, 16 * 5)
            pe.wait_ge(w_low, 4)

            def split_product(o, k, left, right):
                (lh, ll), (rh, rl) = left, right
                for n, (x, y) in enumerate(((lh, rh), (lh, rl), (ll, rh))):
                    last = mm(o, x, y, k == 0 and n == 0, k == KD - 1 and n == 2)
                return last

            def count(s):
                if isinstance(s, int) and s < 2:
                    return
                wait(pe, osum_set, s - 1)
                wait(pe, xtT_taken, KD * (s - 1))
                for j in range(J):
                    o = bank[5][:, j * E:(j + 1) * E]
                    mm(o, strict[:, :], osum[:, j, :], True, False)
                    for i in range(j):
                        mm(o, ones[:, :], osum[:, i, :], False, False)
                    last = mm(o, ones[:, :], oacc[:, :], False, True)
                last.then_inc(cnt_full, 1)

            def step(s, par, first, second, ahead, seq):
                p = s - 1

                def in_product(o, col, w):
                    t = slice(col, col + w)
                    for k in range(KD):
                        last = split_product(o[0:w, :], k, (Winh[:, k, t], Winl[:, k, t]), (x2h[:, k, :], x2l[:, k, :]))
                    return last

                def glu(j):
                    if not second:
                        return
                    w = HW[j]
                    if j == 0:
                        pe.wait_ge(winout_low, KD + 2)
                        wait(pe, x2T_taken, KD * s)
                        wait(pe, x2l_set, KD * s)
                        if first:
                            wait(pe, gate_taken, KD * (s + 1))
                        else:
                            wait(pe, lg_taken, p)
                            wait(pe, cnt_taken, p)
                    wait(pe, u_taken, NH * p + j)
                    in_product(bank[4], j * P, w).then_inc(u_full, 1)
                    wait(pe, prod_set, NH * p + j)
                    in_product(bank[5], HID + j * P, w).then_inc(g_full, 1)

                def score(c, q):
                    if q == 0:
                        wait(pe, kX_set, 16 * s + 4 * (c + 1))
                    if c == 0:
                        if q < 2:
                            wait(pe, v_taken, 2 * s + q + 1)
                        else:
                            wait(pe, kt_taken, 2 * s + q - 1)
                    else:
                        wait(pe, sc_masked, 16 * s + 4 * (c - 1) + q + 1)
                    rows_ = slice(64 * (q % 2), 64 * (q % 2) + 64)
                    t = slice(c * P, (c + 1) * P)
                    for n in range(4):
                        last = mm(bank[q][:, n * P:(n + 1) * P], kX[rows_, c % 2, n, q // 2, :], qT[rows_, q // 2, t], True, True)
                    last.then_inc(sc_full, 1)

                def chunk(c):
                    t = slice(c * P, (c + 1) * P)
                    empty_state = par == 0 and c == 0
                    if c > 0:
                        wait(pe, ret_taken, J * s + c)
                    if not empty_state:
                        wait(pe, state_set, J * s + c)
                        for m in range(KD):
                            mm(bank[6][:, m * P:(m + 1) * P], qT[:, m, t], state[:, m * P:(m + 1) * P], m == 0, False, True)
                    for m in range(KD):
                        last = mm(bank[7][:, m * P:(m + 1) * P], ktok[:, c, m * P:(m + 1) * P], own_columns(c, 2 * m, 2),
                                  True, True)
                    last.then_inc(kv_full, 1)
                    for q in range(4):
                        wait(pe, sc_masked, 16 * s + 4 * c + q + 1)
                        for n in range(4):
                            h = 4 * q + n
                            last = mm(bank[6][:, h // 4 * 64:h // 4 * 64 + 64], sm[:, q, n, :], vz[:, c, h * 64:h * 64 + 64],
                                      empty_state and q == 0 and n == 0, q == 3 and n == 3, True)
                        if q == 3:
                            last.then_inc(ret_full, 1)
                        if c < J - 1:
                            score(c + 1, q)

                if first:
                    wait(pe, xT_taken, KD * (s + 1))
                    wait(pe, xnl_set, KD * (s + 1))
                    for n in range(4):
                        (high, low), m = ((Wqh, Wql), (Wkh, Wkl))[n // 2], n % 2
                        t = slice(m * P, (m + 1) * P)
                        if n == 0:
                            wait(pe, gnT_taken, KD * s)
                        if n == 2:
                            wait(pe, wo_taken, 2 * s)
                        if n == 3:
                            count(s)
                        for k in range(KD):
                            last = split_product(bank[n][:, :], k, (high[:, k, t], low[:, k, t]), (xnh[:, k, :], xnl[:, k, :]))
                        last.then_inc(qk_full, 1)
                if second:
                    wait(pe, x2n_set, s)
                    for k in range(KD):
                        for j in range(J):
                            last = pe.transpose(bank[6 + k][:, j * P:(j + 1) * P], x2n[:, j, k * P:(k + 1) * P], ident)
                        last.then_inc(x2T_full, 1)
                if not first:
                    count(s)
                if first:
                    wait(pe, lg_taken, p)
                    wait(pe, cnt_taken, p)
                    for m in range(KD):
                        for k in range(KD):
                            t = slice(m * P, (m + 1) * P)
                            last = split_product(bank[4 + m][:, :], k, (Wgh[:, k, t], Wgl[:, k, t]), (xnh[:, k, :], xnl[:, k, :]))
                        last.then_inc(gate_full, 1)
                    for i in range(2):
                        wait(pe, qk_taken, 4 * s + i + 1)
                        for jj in range(2):
                            j = 2 * i + jj
                            for k in range(KD):
                                t = slice(j * P, (j + 1) * P)
                                last = split_product(bank[i][:, jj * D:(jj + 1) * D], k, (xnh[:, k, t], xnl[:, k, t]),
                                                     (Wvh[:, k, :], Wvl[:, k, :]))
                        last.then_inc(v_full, 1)
                    wait(pe, qk_taken, 4 * s + 4)
                    for i in range(2):
                        for jj in range(2):
                            j = 2 * i + jj
                            for m in range(KD):
                                last = pe.transpose(bank[2 + i][:, jj * D + m * P:jj * D + (m + 1) * P],
                                                    kT[:, m, j * P:(j + 1) * P], ident)
                        last.then_inc(kt_full, 1)
                glu(0)
                if first:
                    for q in range(4):
                        score(0, q)
                    if second:
                        wait(pe, x2T_taken, KD * s)
                    wait(pe, kt_taken, 2 * (s + 1))
                    wait(pe, v_taken, 2 * (s + 1))
                for c in range(J):
                    if c < J - 1:
                        glu(c + 1)
                    if first:
                        chunk(c)
                glu(NH - 2)
                glu(NH - 1)
                def ffn_out(i):
                    if not second:
                        return
                    if i == 0:
                        wait(pe, u_taken, NH * s)
                    order = [(jj, n) for jj in range(2) for n in range(NH - 1)] + [(jj, NH - 1) for jj in range(2)]
                    for jj, n in order:
                        j, w = 2 * i + jj, HW[n]
                        if j == 0:
                            wait(pe, prodl_set, NH * p + n + 1)
                        t = slice(j * P, (j + 1) * P)
                        for m, (x, y) in enumerate(((prodh[0:w, n, t], Wouth[0:w, n, :]), (prodh[0:w, n, t], Woutl[0:w, n, :]),
                                                    (prodl[0:w, n, t], Wouth[0:w, n, :]))):
                            last = mm(bank[4 + i][:, jj * D:(jj + 1) * D], x, y, jj == 0 and n == 0 and m == 0,
                                      jj == 1 and n == NH - 1 and m == 2, True)
                    last.then_inc(o_full, 1)
                ffn_out(0)
                if first:
                    wait(pe, gn_set, NN * (s + 1))
                    wait(pe, sc_masked, 16 * (s + 1))
                    for m in range(KD):
                        for j in range(J):
                            last = pe.transpose(bank[m][:, j * P:(j + 1) * P], gn[:, j, m * P:(m + 1) * P], ident)
                        last.then_inc(gnT_full, 1)
                ffn_out(1)

                def out_proj(j):
                    if not first:
                        return
                    wait(pe, gg_set, KD * (s + 1))
                    for m in range(KD):
                        last = mm(bank[2 + j // 2][:, j % 2 * D:(j % 2 + 1) * D], gnT[:, m, j * P:(j + 1) * P], Wo[:, m, :],
                                  m == 0, m == KD - 1)
                    if j % 2:
                        last.then_inc(wo_full, 1)

                out_proj(0)
                if ahead:
                    xT(s + 1)
                out_proj(1)
                out_proj(2)
                if second:
                    wait(pe, xt_set, 2 * s)
                    wait(pe, hf_set, 2 * s)
                    for k in range(KD):
                        for j in range(J):
                            last = pe.transpose(bank[4 + k][:, j * P:(j + 1) * P], pl[:, j, 0, k * P:(k + 1) * P], ident)
                        last.then_inc(xtT_full, 1)
                out_proj(3)
                if second:
                    wait(pe, xtT_taken, KD * s)
                    for j in range(J):
                        for k in range(KD):
                            last = mm(bank[4][:, j * E:(j + 1) * E], xtT[:, k, j * P:(j + 1) * P], Gw[:, k, :], k == 0, k == KD - 1)
                    last.then_inc(lg_full, 1)
            steps(pe, step)
            count(G + 1)

            def part(e, b, first, last, n):
                def to_features(e, b, n):
                    wait(pe, xr_in[b], 16 * n)
                    wait(pe, yt_taken, SJ * (e - 1) if not first or e else 0)
                    for k in range(KD):
                        for j in range(SJ):
                            ins = pe.transpose(bank[4 + k][:, j * SP_:(j + 1) * SP_], xr[b][:, j, k * P:(k + 1) * P],
                                               const[0:SP_, K_ID:K_ID + SP_])
                        ins.then_inc(xeT_full, 1)

                def to_tokens(e):
                    wait(pe, y_taken, KD * (e + 1))
                    wait(pe, xel_set, KD * (e + 2) if not last or not same(e) else KD * E)
                    for j in range(SJ):
                        for k in range(KD):
                            ins = pe.transpose(bank[4 + j // 2][0:SR[j], (j % 2) * D + k * P:(j % 2) * D + (k + 1) * P],
                                               yT[:, k, j * SP_:j * SP_ + SR[j]], ident)
                        ins.then_inc(yt_full, 1)

                def same(x):
                    return isinstance(x, int) and x == E - 1

                def product(o, high, low, n, steps):
                    for k in range(steps):
                        n(k)
                        (ah, bh), (al, bl) = high(k), low(k)
                        for t, (x, y) in enumerate(((ah, bh), (ah, bl), (al, bh))):
                            ins = mm(o, x, y, k == 0 and t == 0, k == steps - 1 and t == 2)
                    return ins

                if first:
                    to_features(0, 0, 1)
                wait(pe, w1l_set, KD * (e + 1))
                wait(pe, xel_set, KD * (e + 1))
                for m in range(MF):
                    wait(pe, h1_taken, MF * e + m - 3 if m > 3 or not first else 0)
                    t = slice(m * P, (m + 1) * P)
                    product(bank[m % 4][:, 0:C], lambda k: (W1h[:, k, t], xeh[:, k, :]),
                            lambda k: (W1l[:, k, t], xel[:, k, :]), lambda k: None, KD).then_inc(h1_full, 1)
                    if m == 3 and not first:
                        to_tokens(e - 1)

                def second_operands(m):
                    wait(pe, (w2l_set, w2l_also)[m // (MF // 2)], e + 1)
                    wait(pe, hel_set, MF * e + m + 1)

                for k in range(KD):
                    if k == 1 and not last:
                        to_features(e + 1, 1 - b, n if b == 0 else n + 1)
                    t = slice(k * P, (k + 1) * P)
                    wait(pe, y_taken, KD * e)
                    product(bank[6 + k][:, 0:C], lambda m: (W2h[:, m, t], heh[:, m, :]),
                            lambda m: (W2l[:, m, t], hel[:, m, :]),
                            second_operands if k == 0 else lambda m: None, MF).then_inc(y_full, 1)
                if last:
                    to_tokens(e)

            experts(pe, part)


def kernel(**x):
    import concourse.bacc as _bacc
    from concourse.bass_utils import run_bass_kernel_spmd as _run

    def get(name):
        return np.asarray(x[name])

    def columns(a, n):
        a = np.concatenate([a, np.zeros(n * P - a.shape[0], a.dtype)])
        return a.reshape(n, P).T

    A, M = "L0_attn_", "L0_ffn_"
    consts, positions, empty = shape_constants()
    b_in = get(A + "b_in")
    vecs = np.concatenate(
        [columns(get(A + n), KD) for n in ("norm1_w", "norm1_b", "bq", "bk", "bg", "gn_w", "gn_b", "norm2_w", "norm2_b")]
        + [columns(b_in[:HID], NH), columns(b_in[HID:], NH)], axis=1)
    arrays = {
        "idx": get("x").reshape(G, J, P).transpose(0, 2, 1),
        "emb": get("L0_tok_emb_table"),
        "consts": consts, "positions": positions.astype(np.float32), "empty": empty, "vecs": vecs,
        "rows": np.stack([get(A + n) for n in ("bv", "bo", "b_out")]),
        **{n: get(A + n) for n in ("wq", "wk", "wv", "wg", "wo", "w_in", "w_out")},
        "gate_w": get(M + "gate_w"), "gate_b": get(M + "gate_b"),
        "w1": get(M + "w1").reshape(E, KD, P, F).transpose(0, 2, 1, 3),
        "b1": get(M + "b1").reshape(E, MF, P).transpose(2, 0, 1),
        "w2": get(M + "w2").reshape(E, MF, P, D).transpose(0, 2, 1, 3),
        "b2": get(M + "b2").reshape(E, KD, P).transpose(2, 0, 1),
    }
    arrays = {n: np.ascontiguousarray(v) for n, v in arrays.items()}
    nc = _bacc.Bacc("TRN2", target_bir_lowering=False, num_devices=1)
    args = [nc.dram_tensor(n, v.shape, mybir.dt.from_np(v.dtype), kind="ExternalInput").ap() for n, v in arrays.items()]
    out = nc.dram_tensor("out", [T + DUMP, D], f32, kind="ExternalOutput").ap()
    xe = nc.dram_tensor("xe", [E * CP, ROW], f32, kind="Internal").ap()
    build(nc, *args, out, xe)
    r = _run(nc, [arrays], core_ids=[0])
    return r.results[0]["out"][:T].reshape(B, S, D)
```
